# Optimizing a Trainium2 kernel written in Bass

```python
import numpy as np
import jax
import jax.numpy as jnp

def _softmax(x, axis=-1):
    return jax.nn.softmax(x, axis=axis)
def _gelu(x):
    return jax.nn.gelu(x, approximate=True)
def _silu(x):
    return jax.nn.silu(x)
def _sigmoid(x):
    return jax.nn.sigmoid(x)
def _layernorm(x, axis=-1, eps=1e-5):
    m = jnp.mean(x, axis=axis, keepdims=True)
    v = jnp.var(x, axis=axis, keepdims=True)
    return (x - m) / jnp.sqrt(v + eps)
def _scatter_add(tgt, idx, src, axis=0):
    return tgt.at[idx].add(src)
def _segment_sum(src, seg, n):
    return jax.ops.segment_sum(src, seg, n)

kernel_name = 'mk_adj_resnorm_d1_adj_256_d23f6e'

def setup_inputs(seed: int = 0):
    np.random.seed(seed)
    _w = jnp.asarray
    def _rec_inputs():
        import jax
        import jax.numpy as jnp
        _gk = jax.random.key(seed)
        x = -0.0002928 + 1 * jax.random.normal(jax.random.fold_in(_gk, 1), (16, 1024, 256), jnp.float32)
        _a = jax.random.bernoulli(jax.random.fold_in(_gk, 2), 0.03125, (1024, 1024))
        _a = jnp.logical_or(_a, jnp.swapaxes(_a, -1, -2))
        _a = jnp.logical_or(_a, jnp.eye(1024, dtype=bool))
        adj = _a.astype(jnp.int32)
        return x, adj
    x, adj = _rec_inputs()
    def _L0_gnn_setup():
        import jax, jax.numpy as jnp
        import numpy as np
        ALPHA = 0.2
        NEG_INF = -9000000000000000.0

        def _gat(inp, adj_mask, W, a):
            h = jnp.matmul(inp, W)
            F_ = h.shape[-1]
            f1 = jnp.matmul(h, a[:F_, 0])
            f2 = jnp.matmul(h, a[F_:, 0])
            e = jax.nn.leaky_relu(f1[:, :, None] + f2[:, None, :], ALPHA)
            if adj_mask is not None:
                e = jnp.where(adj_mask[None, :, :] > 0, e, NEG_INF)
            att = jax.nn.softmax(e, axis=2)
            h_prime = jnp.einsum('bij,bjf->bif', att, h)
            return jax.nn.elu(h_prime)
        key = jax.random.key(seed)
        ks = jax.random.split(key, 10)
        B, N, Fin, H, O = (16, 1024, 256, 512, 256)

        def xavier(k, shape):
            fan_in, fan_out = (shape[0], shape[-1])
            bound = 1.414 * np.sqrt(6.0 / (fan_in + fan_out))
            return jax.random.uniform(k, shape, jnp.float32, -bound, bound)
        return {'x': jax.random.normal(ks[0], (B, N, Fin), jnp.float32), 'adj': jax.random.randint(ks[1], (N, N), 0, 2, jnp.int32), 'mlp1_w': xavier(ks[2], (Fin, H)), 'mlp1_b': jnp.zeros((H,), jnp.float32), 'mlp2_w': xavier(ks[3], (H, O)), 'mlp2_b': jnp.zeros((O,), jnp.float32), 'W_fc': xavier(ks[4], (H, H)), 'a_fc': xavier(ks[5], (2 * H, 1)), 'W_hand': xavier(ks[6], (O, O)), 'a_hand': xavier(ks[7], (2 * O, 1))}
    _L0_gnn_all = _L0_gnn_setup()
    _L0_gnn_in = {k: v for k, v in _L0_gnn_all.items() if k in ('mlp1_w', 'mlp1_b', 'mlp2_w', 'mlp2_b', 'W_fc', 'a_fc', 'W_hand', 'a_hand', )}
    del _L0_gnn_all

    return {
        "x": x,
        "adj": adj,
        "L0_gnn_mlp1_w": _L0_gnn_in["mlp1_w"],
        "L0_gnn_mlp1_b": _L0_gnn_in["mlp1_b"],
        "L0_gnn_mlp2_w": _L0_gnn_in["mlp2_w"],
        "L0_gnn_mlp2_b": _L0_gnn_in["mlp2_b"],
        "L0_gnn_W_fc": _L0_gnn_in["W_fc"],
        "L0_gnn_a_fc": _L0_gnn_in["a_fc"],
        "L0_gnn_W_hand": _L0_gnn_in["W_hand"],
        "L0_gnn_a_hand": _L0_gnn_in["a_hand"],
    }

def reference(x, adj, L0_gnn_mlp1_w, L0_gnn_mlp1_b, L0_gnn_mlp2_w, L0_gnn_mlp2_b, L0_gnn_W_fc, L0_gnn_a_fc, L0_gnn_W_hand, L0_gnn_a_hand):
    import jax
    import jax.numpy as jnp
    def _L0_gnn_ref(x, adj, mlp1_w, mlp1_b, mlp2_w, mlp2_b, W_fc, a_fc, W_hand, a_hand):
        import jax, jax.numpy as jnp
        import numpy as np
        ALPHA = 0.2
        NEG_INF = -9000000000000000.0

        def _gat(inp, adj_mask, W, a):
            h = jnp.matmul(inp, W)
            F_ = h.shape[-1]
            f1 = jnp.matmul(h, a[:F_, 0])
            f2 = jnp.matmul(h, a[F_:, 0])
            e = jax.nn.leaky_relu(f1[:, :, None] + f2[:, None, :], ALPHA)
            if adj_mask is not None:
                e = jnp.where(adj_mask[None, :, :] > 0, e, NEG_INF)
            att = jax.nn.softmax(e, axis=2)
            h_prime = jnp.einsum('bij,bjf->bif', att, h)
            return jax.nn.elu(h_prime)
        out = jax.nn.relu(jnp.matmul(x, mlp1_w) + mlp1_b)
        residual = out
        out = _gat(jax.nn.relu(out), None, W_fc, a_fc)
        out = jax.nn.elu(out) + residual
        out = jax.nn.relu(jnp.matmul(out, mlp2_w) + mlp2_b)
        residual = out
        out = _gat(jax.nn.relu(out), adj, W_hand, a_hand)
        out = jax.nn.elu(out) + residual
        return jax.nn.relu(out)

    x = _layernorm(x + _L0_gnn_ref(x, adj, L0_gnn_mlp1_w, L0_gnn_mlp1_b, L0_gnn_mlp2_w, L0_gnn_mlp2_b, L0_gnn_W_fc, L0_gnn_a_fc, L0_gnn_W_hand, L0_gnn_a_hand), axis=-1)
    return x


_drawn_inputs = setup_inputs


def setup_inputs(seed=0):
    import zlib

    import numpy as np

    out = dict(_drawn_inputs(seed))
    spreads = {'L0_gnn_mlp1_b': (0.0, 0.1), 'L0_gnn_mlp2_b': (0.0, 0.1)}
    factors = {}
    for name, (base, spread) in spreads.items():
        noise = np.random.default_rng([zlib.crc32(name.encode()), seed]).standard_normal(out[name].shape)
        drawn = base * np.exp(spread * noise) if base else spread * noise
        out[name] = jnp.asarray(drawn.astype(out[name].dtype))
    for name, factor in factors.items():
        out[name] = (out[name] * factor).astype(out[name].dtype)
    return out
```

```python
from contextlib import ExitStack

import concourse.bass as bass
from concourse import mybir

F32 = mybir.dt.float32
F32R = mybir.dt.float32r
BF16 = mybir.dt.bfloat16
I32 = mybir.dt.int32
U8 = mybir.dt.uint8
ALU = mybir.AluOpType
ACT = mybir.ActivationFunctionType
AX = mybir.AxisListType
ALL_MAX = bass.bass_isa.ReduceOp.max

P = 128
BANK = 512
SLOPE = 0.2
NEG_INF = -9000000000000000.0
RATIO_CAP = 75.0
LN_EPS = 1e-5

ATT1_BANKS = ((0, 1, 2, 3), (4, 5, 6, 7))
SUM_BANK = (4, 0)
MLP2_BANKS = ((1, 2), (6, 7))
ATT2_BANKS = ((3, 0, 4, 5), (1, 2, 6, 7))
XT_BANKS = ((1, 2), (3, 0))
MLP1_BANKS = ((1, 2, 6, 7), (3, 0, 4, 5))
ROLL_BANKS = (3, 0, 4, 5)
KEY2_BANK, KEY1_BANK = 1, 2
ROW_A, ROW_B = 1, 6


def pipelined(first, second, half, n):
    steps = [(first, half, 0)]
    for j in range(n):
        if j + 1 < n:
            steps.append((first, half, j + 1))
        steps.append((second, half, j))
    return steps


def merged(main, other):
    out, k = [], 0
    for n, step in enumerate(main):
        out.append(step)
        while k < len(other) and (k + 1) * len(main) <= (n + 1) * len(other):
            out.append(other[k])
            k += 1
    return out + other[k:]


def staged(kinds, half, n):
    out = []
    for turn in range(n + len(kinds) - 1):
        for s, kind in reversed(list(enumerate(kinds))):
            if 0 <= turn - s < n:
                out.append((kind, half, turn - s))
    return out


POST = ("normalise1", "clamp1", "residual1")
FINAL = ("normalise2", "clamp2", "residual2")


def plan_attention(nj, second):
    steps = [("sum1", 0, 0)] + pipelined("weigh1", "split1", 1, nj)
    if second:
        steps += merged(pipelined("weigh2", "split2", 0, nj), staged(POST, 0, 4) + [("sum1", 1, 0)])
        steps += staged(POST, 1, 4)[:6] + [("relu2", 0, 0), ("relu2", 0, 1)] + staged(POST, 1, 4)[6:]
        steps += merged(pipelined("weigh2", "split2", 1, nj), staged(FINAL, 0, 4))
        steps += [("scale2", 0, 0)]
    else:
        steps += staged(POST, 0, 4) + [("sum1", 1, 0)] + staged(POST, 1, 4)
        steps += [("relu2", 0, 0), ("relu2", 0, 1)]
    return steps


def links_of(steps):
    each = {"weigh2": 1, "residual1": 1, "normalise2": 1, "residual2": 4, "keys1": 1, "keys2": 3,
            "rows2": 5}
    return sum(each.get(kind, 0) for kind, _, _ in steps)


def build(nc, x, adj, w1, b1, w2, b2, wf, af, wh, ah, out):
    NB, N, FI = x.shape
    H = w1.shape[1]
    O = w2.shape[1]
    KI, KH, KO, NT = FI // P, H // P, O // P, N // P
    NH = N // BANK
    TH = NT // NH
    ONES = 2
    assert FI == O and NH == 2 and KH == 4 and KO == 2 and KI == 2 and NT == 8 and NB >= 3

    with ExitStack() as ctx:
        def sb(name, shape, dt):
            return ctx.enter_context(nc.sbuf_tensor(name, shape, dt))

        def sem(name):
            return ctx.enter_context(nc.semaphore(name))

        w1_sb = sb("w1_sb", [P, KI, H], F32)
        wf_sb = sb("wf_sb", [P, KH, H], F32)
        w2_sb = sb("w2_sb", [P, KH, O], F32)
        wh_sb = sb("wh_sb", [P, KO, O], F32)
        b1_sb = sb("b1_sb", [P, KH], F32)
        b2_sb = sb("b2_sb", [P, KO], F32)
        v1_sb = sb("v1_sb", [P, KH, 2], F32)
        v2_sb = sb("v2_sb", [P, KO, 2], F32)
        adj_sb = sb("adj_sb", [P, NT, N], U8)
        hidden = sb("hidden", [P, NT, N], U8)
        ident = sb("ident", [P, P], F32)
        neg_one = sb("neg_one", [P, 1], F32)
        ones = sb("ones", [P, P], F32)
        neg_half = sb("neg_half", [P, TH], F32)

        x_in = sb("x_in", [P, TH, FI], F32)
        x_t = sb("x_t", [P, KI, N], F32)
        act1 = sb("act1", [P, KH, N], F32)
        h_hi = sb("h_hi", [P, NT, H], F32R)
        h_lo = sb("h_lo", [P, NT, H], F32R)
        act2_t = sb("act2_t", [P, KO, N], F32)
        act2 = sb("act2", [P, NT, O], F32)
        h2_hi = sb("h2_hi", [P, NT, O + ONES], F32R)
        h2_lo = sb("h2_lo", [P, NT, O], F32R)
        y = sb("y", [P, NH, TH, O], F32)

        p_hi = sb("p_hi", [P, NT, BANK], F32R)
        p_lo = sb("p_lo", [P, NT, BANK], F32R)
        p_full = sb("p_full", [P, 3, BANK], F32)
        p_sum = sb("p_sum", [P, BANK], F32)
        rsum1 = sb("rsum1", [P, BANK], F32)
        ratio = sb("ratio", [P, N], F32)
        alpha = sb("alpha", [P, N], F32)
        beta = sb("beta", [P, N], F32)
        u1 = sb("u1", [P, 2, BANK], F32)
        e1 = sb("e1", [P, 2, BANK], F32)
        u2 = sb("u2", [P, 3, O], F32)
        e2 = sb("e2", [P, 2, O], F32)
        junk = sb("junk", [P, N], U8)

        keys1 = sb("keys1", [P, NT, 2], F32)
        keys2 = sb("keys2", [P, NT, 2], F32)
        top1 = sb("top1", [P, 1], F32)
        top1_all = sb("top1_all", [P, 1], F32)
        neg_top = sb("neg_top", [P, 2], F32)
        gap = sb("gap", [P, NT], F32)
        key_exp = sb("key_exp", [P, 2, NT], F32)
        neg_key = sb("neg_key", [P, NT], F32)
        low2 = sb("low2", [P, 1], F32)
        low2_all = sb("low2_all", [P, 1], F32)
        lift = sb("lift", [P, 1], F32)
        key_pos = sb("key_pos", [P, NT], F32)
        seen = sb("seen", [P, NT], F32)
        lone = sb("lone", [P, NT], F32)
        best = sb("best", [P, NT], F32)
        top2 = sb("top2", [P, NT], F32)
        alpha_col = sb("alpha_col", [P, NT], F32)
        beta_col = sb("beta_col", [P, NT], F32)
        slope_key = sb("slope_key", [P, NT], F32)
        rsum2 = sb("rsum2", [P, 2], F32)
        stats = sb("stats", [P, 2, 6], F32)
        moments = sb("moments", [P, TH, 2], F32)
        var_eps = sb("var_eps", [P, TH], F32)
        rstd = sb("rstd", [P, TH], F32)

        ps = ctx.enter_context(nc.psum_tensor("ps", [P, 8, BANK], F32))

        w_loaded, a_loaded = sem("w_loaded"), sem("a_loaded")
        adj_loaded = [sem("adj_loaded0"), sem("adj_loaded1")]
        x_loaded = [sem("x_loaded0"), sem("x_loaded1")]
        y_loaded = [sem("y_loaded0"), sem("y_loaded1")]
        y_stored = [sem("y_stored0"), sem("y_stored1")]
        zeroed, consts, ident_set = sem("zeroed"), sem("consts"), sem("ident_set")
        a_used, keys_set, ones_set = sem("a_used"), sem("keys_set"), sem("ones_set")
        adj_seen, adj_turned, adj_used = sem("adj_seen"), sem("adj_turned"), sem("adj_used")
        xt_done, mlp1_done, keys1_done, h_done = sem("xt_done"), sem("mlp1_done"), sem("keys1_done"), sem("h_done")
        sum1_done, mlp2_done = sem("sum1_done"), sem("mlp2_done")
        res_done, h2_done, keys2_done = sem("res_done"), sem("h2_done"), sem("keys2_done")
        gap_spread, row_done = sem("gap_spread"), sem("row_done")
        p1_used, p2_used = sem("p1_used"), sem("p2_used")
        xt_ready, act1_ready = sem("xt_ready"), sem("act1_ready")
        h_hi_ready, h_ready = sem("h_hi_ready"), sem("h_ready")
        keys1_read, top1_ready, top1_shared = sem("keys1_read"), sem("top1_ready"), sem("top1_shared")
        gap_ready, exp_ready, ratio_ready = sem("gap_ready"), sem("exp_ready"), sem("ratio_ready")
        p1_full, p1_hi, p1_ready = sem("p1_full"), sem("p1_hi"), sem("p1_ready")
        waited_pool, waited_dve = sem("waited_pool"), sem("waited_dve")
        rsum_ready, p1_summed, seen_set = sem("rsum_ready"), sem("p1_summed"), sem("seen_set")
        normed, e1_ready, clamped1, e1_done, post_done = (
            sem("normed"), sem("e1_ready"), sem("clamped1"), sem("e1_done"), sem("post_done"))
        act2_ready, res_ready, h2_hi_ready, h2_ready = (
            sem("act2_ready"), sem("res_ready"), sem("h2_hi_ready"), sem("h2_ready"))
        keys2_read, low2_ready, low2_shared, pos_ready = (
            sem("keys2_read"), sem("low2_ready"), sem("low2_shared"), sem("pos_ready"))
        cols_ready, rows_ready = sem("cols_ready"), sem("rows_ready")
        p2_slope, p2_masked, p2_full, p2_hi, p2_ready = (
            sem("p2_slope"), sem("p2_masked"), sem("p2_full"), sem("p2_hi"), sem("p2_ready"))
        part2_ready, e2_ready, att2_read, e2_done, moments_ready = (
            sem("part2_ready"), sem("e2_ready"), sem("att2_read"), sem("e2_done"), sem("moments_ready"))
        var_ready, rstd_ready, y_ready, dve_link = (
            sem("var_ready"), sem("rstd_ready"), sem("y_ready"), sem("dve_link"))

        class Turn:

            def __init__(self, eng, b):
                self.eng, self.b, self.times = eng, b, {}

            def __call__(self, per, n, ahead=0):
                if isinstance(self.b, int):
                    return (self.b + ahead) * per + n
                if per not in self.times:
                    self.times[per] = self.eng.snap(self.b * per)
                return self.times[per] + (ahead * per + n)

        STEADY = plan_attention(NT, True)
        NEXT_A = [("split_xt", 0, 0), ("split_xt", 0, 1), ("relu2", 1, 0), ("relu2", 1, 1),
                  ("split_xt", 1, 0), ("split_xt", 1, 1)]
        NEXT_A += [("relu1", h, f) for h in range(NH) for f in range(KH)]

        def tail_plan(second, nxt):
            steps = (NEXT_A if nxt else [("relu2", 1, 0), ("relu2", 1, 1)])
            steps = steps + (staged(FINAL, 1, 4) + [("scale2", 1, 0)] if second else [])
            steps += [("residual", 0, n) for n in range(4)] + [("store_h2", 0, n) for n in range(4)]
            steps += [("keys2", 0, 0)]
            if nxt:
                steps += [("keys1", 0, 0), ("store_h", 0, 0), ("store_h", 0, 1), ("gap1", 0, 0)]
                steps += [("lift2", 0, 0), ("store_h", 0, 2), ("store_h", 0, 3)]
                seen_steps = [("seen2", 0, t) for t in range(NT)]
                more = [("store_h", 0, t) for t in range(4, NT)]
                steps += merged(seen_steps, more) + [("rows2", 0, 0)]
                steps += pipelined("weigh1", "split1", 0, NT)[:8]
                steps += [("spread2", 0, 0)]
                steps += pipelined("weigh1", "split1", 0, NT)[8:]
            else:
                steps += [("lift2", 0, 0)] + [("seen2", 0, t) for t in range(NT)]
                steps += [("rows2", 0, 0), ("spread2", 0, 0)]
            return steps

        FRONT = [("split_xt", h, k) for h in range(NH) for k in range(KI)]
        FRONT += [("relu1", h, f) for h in range(NH) for f in range(KH)]
        FRONT += [("keys1", 0, 0)] + [("store_h", 0, t) for t in range(2)] + [("gap1", 0, 0)]
        FRONT += [("store_h", 0, t) for t in range(2, NT)] + pipelined("weigh1", "split1", 0, NT)
        LAST = pipelined("weigh2", "split2", 0, NT)
        LAST += merged(pipelined("weigh2", "split2", 1, NT), staged(FINAL, 0, 4))
        LAST += [("scale2", 0, 0)] + staged(FINAL, 1, 4) + [("scale2", 1, 0)]

        def whole(second, nxt):
            return plan_attention(NT, second) + tail_plan(second, nxt)

        LINKS_FRONT = links_of(FRONT)
        LINKS_FIRST = links_of(whole(False, True))
        LINKS = links_of(whole(True, True))

        def nodes(h):
            return slice(h * BANK, (h + 1) * BANK)

        def block_of(n):
            return slice(n * P, (n + 1) * P)

        x_v = x.rearrange("b (h t p) f -> b h p t f", p=P, t=TH)
        out_v = out.rearrange("b (h t p) f -> b h p t f", p=P, t=TH)
        stage = act1[:, 0:2, :].bitcast(I32)
        stage_f = act1[:, 2:4, :]
        a_rows = p_full[:, 0:2, :]
        a2_rows = u1[:, 0:1, :]
        a_junk = e1[:, 0, :]

        block = ctx.enter_context(nc.Block())

        @block.sync
        def _(sp):
            for dst, src in ((w1_sb, w1), (wf_sb, wf), (w2_sb, w2), (wh_sb, wh)):
                sp.dma_start(dst[:], src.rearrange("(k p) f -> p k f", p=P)).then_inc(w_loaded, 16)
            with nc.allow_non_contiguous_dma(reason="biases, a few hundred elements, once"):
                sp.dma_start(b1_sb[:], b1.rearrange("(k p) -> p k", p=P)).then_inc(w_loaded, 16)
                sp.dma_start(b2_sb[:], b2.rearrange("(k p) -> p k", p=P)).then_inc(w_loaded, 16)
            a_row = af.rearrange("(s f) c -> (c s) f", s=2)
            a2_row = ah.rearrange("(s f) c -> c (s f)", s=2)
            for s in range(2):
                sp.dma_start(a_rows[:, s, :], a_row[s:s + 1, :].to_broadcast([P, H])).then_inc(a_loaded, 16)
            sp.dma_start(a2_rows[:, 0, :], a2_row[0:1, :].to_broadcast([P, 2 * O])).then_inc(a_loaded, 16)
            for t in range(NT):
                if t >= 2:
                    sp.wait_ge(adj_seen, 2 * (t - 1))
                sp.dma_start(stage[:, t % 2, :], adj[t * P:(t + 1) * P, :]).then_inc(adj_loaded[t % 2], 16)

            def load_x(T, b, ahead):
                for h in range(NH):
                    n = T(4, 2 * h, ahead)
                    if not isinstance(n, int) or n > 0:
                        sp.wait_ge(xt_done, n)
                    sp.dma_start(x_in[:], x_v[b + ahead, h]).then_inc(x_loaded[h], 16)

            def pass_y(T, b, first):
                for h in range(NH):
                    if not first:
                        sp.wait_ge(y_stored[h], T(16, 0, -1))
                    sp.dma_start(y[:, h], x_v[b - 1, h]).then_inc(y_loaded[h], 16)

            def store_y(T, b, h):
                sp.wait_ge(y_ready, T(2, h + 1, -1))
                sp.dma_start(out_v[b - 1, h], y[:, h]).then_inc(y_stored[h], 16)

            def steady(b, first=False, nxt=True):
                T = Turn(sp, b)
                pass_y(T, b, first)
                store_half(T, b, nxt)

            def store_half(T, b, nxt):
                if nxt:
                    for h in range(NH):
                        sp.wait_ge(xt_done, T(4, 2 * h, 1))
                        sp.dma_start(x_in[:], x_v[b + 1, h]).then_inc(x_loaded[h], 16)
                for h in range(NH):
                    store_y(T, b, h)

            load_x(Turn(sp, 0), 0, 0)
            load_x(Turn(sp, 0), 0, 1)
            steady(1, first=True)
            with sp.Fori(2, NB - 1) as b:
                steady(b)
            steady(NB - 1, nxt=False)
            steady(NB, nxt=False)
            for h in range(NH):
                sp.wait_ge(y_stored[h], 16 * NB)

        @block.gpsimd
        def _(pool):
            pool.memset(ident[:], 0.0).then_inc(zeroed, 1)
            pool.wait_ge(zeroed, 1)
            pool.affine_select(out=ident[:], in_=ident[:], compare_op=ALU.not_equal, fill=1.0, base=0,
                               pattern=[[-1, P]], channel_multiplier=1).then_inc(ident_set, 1)
            pool.memset(neg_half[:], -0.5).then_inc(zeroed, 1)
            pool.wait_ge(zeroed, 2)

            def top(T, ahead):
                pool.wait_ge(top1_ready, T(1, 1, ahead))
                pool.sem_inc(waited_pool)
                pool.partition_all_reduce(top1_all[:], top1[:], P, ALL_MAX).then_inc(top1_shared, 1)

            def low(T):
                pool.wait_ge(low2_ready, T(1, 1))
                pool.sem_inc(waited_pool)
                pool.partition_all_reduce(low2_all[:], low2[:], P, ALL_MAX).then_inc(low2_shared, 1)

            def deviation(T, h):
                pool.wait_ge(var_ready, T(2, h + 1, -1))
                pool.tensor_tensor(rstd[:], var_eps[:], neg_half[:], ALU.pow).then_inc(rstd_ready, 1)

            def iteration(b, second=True, nxt=True):
                T = Turn(pool, b)
                if second:
                    deviation(T, 0)
                    deviation(T, 1)
                low(T)
                if nxt:
                    top(T, 1)

            top(Turn(pool, 0), 0)
            iteration(0, second=False)
            with pool.Fori(1, NB - 1) as b:
                iteration(b)
            iteration(NB - 1, nxt=False)
            T = Turn(pool, NB)
            deviation(T, 0)
            deviation(T, 1)

        @block.tensor
        def _(pe):
            def turn_x(T, ahead, h):
                pe.wait_ge(x_loaded[h], T(16, 16, ahead))
                for k in range(KI):
                    for t in range(TH):
                        last = pe.transpose(ps[:, XT_BANKS[h][k], block_of(t)], x_in[:, t, block_of(k)], ident[:])
                    last.then_inc(xt_done, 1)

            def mlp1(T, ahead, h):
                pe.wait_ge(xt_ready, T(4, 2 * h + 2, ahead))
                for f in range(KH):
                    for k in range(KI):
                        last = pe.matmul(ps[:, MLP1_BANKS[h][f], :], w1_sb[:, k, block_of(f)], x_t[:, k, nodes(h)],
                                         start=(k == 0), stop=(k == KI - 1))
                    last.then_inc(mlp1_done, 1)

            def keys(src, v, n, bank, done):
                for t in range(NT):
                    for k in range(n):
                        last = pe.matmul(ps[:, bank, 2 * t:2 * t + 2], src[:, k, block_of(t)], v[:, k, :],
                                         start=(k == 0), stop=(k == n - 1))
                last.then_inc(done, 1)

            def spread(col, bank, done):
                for t in range(NT):
                    last = pe.matmul(ps[:, bank + t // TH, block_of(t % TH)], col[:, t:t + 1].to_broadcast([P, P]),
                                     ident[:], start=True, stop=True)
                last.then_inc(done, 1)

            def h_tile(T, ahead, t):
                if t >= len(ROLL_BANKS):
                    pe.wait_ge(h_ready, T(8, t - 3, ahead))
                for k in range(KH):
                    last = pe.matmul(ps[:, ROLL_BANKS[t % 4], :], act1[:, k, block_of(t)], wf_sb[:, k, :],
                                     start=(k == 0), stop=(k == KH - 1))
                last.then_inc(h_done, 1)

            def attend1(T, h):
                for j in range(NT):
                    if j == 2 + 3 * h:
                        pe.wait_ge(p1_summed, T(16, 8 * h + 8))
                        if h == 1:
                            pe.wait_ge(normed, T(8, 1))
                        pe.matmul(ps[:, SUM_BANK[h], :], ones[:], p_sum[:], start=True, stop=True).then_inc(sum1_done, 1)
                    if h == 1 and j == 0:
                        pe.wait_ge(rsum_ready, T(2, 1))
                    pe.wait_ge(p1_ready, T(16, 8 * h + j + 1))
                    for f in range(KH):
                        acc = ps[:, ATT1_BANKS[h][f], :]
                        pe.matmul(acc, h_hi[:, j, block_of(f)], p_hi[:, j, :], start=(j == 0), stop=False)
                        pe.matmul(acc, h_hi[:, j, block_of(f)], p_lo[:, j, :], start=False, stop=False)
                        last = pe.matmul(acc, h_lo[:, j, block_of(f)], p_hi[:, j, :], start=False, stop=(j == NT - 1))
                    last.then_inc(p1_used, 1)

            def attend2(T, h):
                for j in range(NT):
                    pe.wait_ge(p2_ready, T(16, 8 * h + j + 1, -1))
                    for q in range(TH):
                        acc = ps[:, ATT2_BANKS[h][q], 0:O + ONES]
                        pe.matmul(acc, p_hi[:, j, block_of(q)], h2_hi[:, j, :], start=(j == 0), stop=False)
                        pe.matmul(acc, p_lo[:, j, block_of(q)], h2_hi[:, j, :], start=False, stop=False)
                        last = pe.matmul(ps[:, ATT2_BANKS[h][q], 0:O], p_hi[:, j, block_of(q)], h2_lo[:, j, :],
                                         start=False, stop=(j == NT - 1))
                    last.then_inc(p2_used, 1)

            def mlp2(T, h):
                pe.wait_ge(post_done, T(8, 4 * h + 4))
                for o in range(KO):
                    for k in range(KH):
                        last = pe.matmul(ps[:, MLP2_BANKS[h][o], :], w2_sb[:, k, block_of(o)], act1[:, k, nodes(h)],
                                         start=(k == 0), stop=(k == KH - 1))
                    last.then_inc(mlp2_done, 1)

            def iteration(b, second=True, nxt=True):
                T = Turn(pe, b)
                pe.wait_ge(h_ready, T(8, 8))
                if second:
                    pe.wait_ge(rows_ready, T(4, 4, -1))
                pe.wait_ge(ratio_ready, T(2, 2))
                attend1(T, 0)
                attend1(T, 1)
                mlp2(T, 0)
                if second:
                    pe.wait_ge(h2_ready, T(4, 4, -1))
                    pe.wait_ge(rsum_ready, T(2, 2))
                    pe.wait_ge(normed, T(8, 6))
                    attend2(T, 0)
                if nxt:
                    pe.wait_ge(act2_ready, T(4, 2))
                    turn_x(T, 1, 0)
                mlp2(T, 1)
                if nxt:
                    if second:
                        pe.wait_ge(att2_read, T(8, 2, -1))
                    else:
                        pe.wait_ge(rsum_ready, T(2, 2))
                    turn_x(T, 1, 1)
                pe.wait_ge(act2_ready, T(4, 4))
                if nxt:
                    mlp1(T, 1, 0)
                    if second:
                        pe.wait_ge(att2_read, T(8, 4, -1))
                    mlp1(T, 1, 1)
                if second:
                    if nxt:
                        pe.wait_ge(act1_ready, T(8, 4, 1))
                    attend2(T, 1)
                if nxt:
                    pe.wait_ge(act1_ready, T(8, 8, 1))
                elif second:
                    pe.wait_ge(att2_read, T(8, 4, -1))
                for n in range(4):
                    for t in (2 * n, 2 * n + 1):
                        for o in range(KO):
                            at = (t % 2) * O + o * P
                            last = pe.transpose(ps[:, ROLL_BANKS[n], at:at + P], act2_t[:, o, block_of(t)], ident[:])
                    last.then_inc(res_done, 1)
                for n in range(4):
                    pe.wait_ge(res_ready, T(4, n + 1))
                    for t in (2 * n, 2 * n + 1):
                        for k in range(KO):
                            last = pe.matmul(ps[:, ROLL_BANKS[n], (t % 2) * O:(t % 2 + 1) * O],
                                             act2_t[:, k, block_of(t)], wh_sb[:, k, :],
                                             start=(k == 0), stop=(k == KO - 1))
                    last.then_inc(h2_done, 1)
                if second:
                    pe.wait_ge(att2_read, T(8, 6, -1))
                keys(act2_t, v2_sb, KO, KEY2_BANK, keys2_done)
                if nxt:
                    keys(act1, v1_sb, KH, KEY1_BANK, keys1_done)
                    for t in range(2):
                        pe.wait_ge(h2_ready, T(4, t + 1))
                        h_tile(T, 1, t)
                    pe.wait_ge(gap_ready, T(1, 1, 1))
                    pe.wait_ge(keys2_read, T(1, 1))
                    spread(gap, ROW_A, gap_spread)
                if second:
                    pe.wait_ge(att2_read, T(8, 8, -1))
                pe.wait_ge(pos_ready, T(1, 1))
                spread(key_pos, ROW_B, row_done)
                if nxt:
                    for t in range(2, NT):
                        if t < 4:
                            pe.wait_ge(h2_ready, T(4, t + 1))
                        h_tile(T, 1, t)
                    pe.wait_ge(ratio_ready, T(2, 2, 1))
                pe.wait_ge(cols_ready, T(1, 1))
                spread(alpha_col, ROW_A, row_done)
                spread(beta_col, ROW_B, row_done)

            pe.wait_ge(ident_set, 1)
            pe.wait_ge(consts, 4)
            for t in range(NT):
                pe.wait_ge(adj_seen, 2 * (t + 1))
                for h in range(NH):
                    if t >= 2:
                        pe.wait_ge(adj_used, 2 * (t - 1) + h - 1)
                    for j in range(TH):
                        last = pe.transpose(ps[:, 4 * (t % 2) + h, block_of(j)],
                                            stage_f[:, t % 2, block_of(h * TH + j)], ident[:])
                    last.then_inc(adj_turned, 1)
            pe.wait_ge(w_loaded, 96)
            pe.wait_ge(keys_set, 12)
            pe.wait_ge(adj_used, 16)
            T = Turn(pe, 0)
            turn_x(T, 0, 0)
            turn_x(T, 0, 1)
            mlp1(T, 0, 0)
            pe.wait_ge(xt_ready, 4)
            mlp1(T, 0, 1)
            pe.wait_ge(act1_ready, 8)
            keys(act1, v1_sb, KH, KEY1_BANK, keys1_done)
            h_tile(T, 0, 0)
            h_tile(T, 0, 1)
            pe.wait_ge(gap_ready, 1)
            spread(gap, ROW_A, gap_spread)
            for t in range(2, NT):
                h_tile(T, 0, t)

            iteration(0, second=False)
            with pe.Fori(1, NB - 1) as b:
                iteration(b)
            iteration(NB - 1, nxt=False)
            T = Turn(pe, NB)
            pe.wait_ge(rows_ready, 4 * NB)
            pe.wait_ge(h2_ready, 4 * NB)
            attend2(T, 0)
            attend2(T, 1)

        @block.scalar
        def _(act):
            act.wait_ge(consts, 4)
            for t in range(NT):
                act.activation(h2_hi[:, t, O:O + ONES], ones[:, 0:ONES], ACT.Copy).then_inc(ones_set, 1)
            act.wait_ge(w_loaded, 96)

            def run(steps, T):
                for kind, h, n in steps:
                    if kind == "split_xt":
                        act.wait_ge(xt_done, T(4, 2 * h + n + 1, 1))
                        act.activation(x_t[:, n, nodes(h)], ps[:, XT_BANKS[h][n], :], ACT.Copy).then_inc(xt_ready, 1)
                    elif kind == "relu1":
                        act.wait_ge(mlp1_done, T(8, 4 * h + n + 1, 1))
                        act.activation(act1[:, n, nodes(h)], ps[:, MLP1_BANKS[h][n], :], ACT.Relu,
                                       bias=b1_sb[:, n:n + 1]).then_inc(act1_ready, 1)
                    elif kind == "store_h":
                        act.wait_ge(h_done, T(8, n + 1, 1))
                        act.activation(h_hi[:, n, :], ps[:, ROLL_BANKS[n % 4], :], ACT.Copy).then_inc(h_hi_ready, 1)
                    elif kind == "gap1":
                        act.wait_ge(gap_ready, T(1, 1, 1))
                        act.activation(key_exp[:, 0, :], keys1[:, :, 1], ACT.Exp, bias=neg_top[:, 0:1])
                        act.activation(key_exp[:, 1, :], keys1[:, :, 1], ACT.Exp, bias=neg_top[:, 1:2],
                                       scale=SLOPE).then_inc(exp_ready, 1)
                        act.wait_ge(gap_spread, T(1, 1, 1))
                        for half in range(NH):
                            act.activation(ratio[:, nodes(half)], ps[:, ROW_A + half, :], ACT.Exp,
                                           scale=1.0 - SLOPE).then_inc(ratio_ready, 1)
                    elif kind == "weigh1":
                        ahead = 1 - h
                        act.wait_ge(p1_full, T(16, 8 * h + n + 1, ahead))
                        if h == 1:
                            act.wait_ge(p1_used, T(16, n + 1))
                        act.activation(p_hi[:, n, :], p_full[:, n % 3, :], ACT.Copy).then_inc(p1_hi, 1)
                    elif kind == "normalise1":
                        act.wait_ge(normed, T(8, 4 * h + n + 1))
                        act.activation(e1[:, n % 2, :], u1[:, n % 2, :], ACT.Exp).then_inc(e1_ready, 1)
                    elif kind == "clamp1":
                        act.wait_ge(clamped1, T(8, 4 * h + n + 1))
                        act.activation(e1[:, n % 2, :], e1[:, n % 2, :], ACT.Exp, bias=neg_one[:]).then_inc(e1_done, 1)
                    elif kind == "relu2":
                        act.wait_ge(mlp2_done, T(4, 2 * h + n + 1))
                        act.activation(act2_t[:, n, nodes(h)], ps[:, MLP2_BANKS[h][n], :], ACT.Relu,
                                       bias=b2_sb[:, n:n + 1]).then_inc(act2_ready, 1)
                    elif kind == "residual":
                        act.wait_ge(res_done, T(4, n + 1))
                        if n == 0 and not first_turn:
                            act.wait_ge(moments_ready, T(8, 8, -1))
                        act.activation(act2[:, 2 * n:2 * n + 2, :],
                                       ps[:, ROLL_BANKS[n], :].rearrange("p (t o) -> p t o", t=2),
                                       ACT.Identity, bias=neg_one[:]).then_inc(res_ready, 1)
                    elif kind == "store_h2":
                        act.wait_ge(h2_done, T(4, n + 1))
                        act.activation(h2_hi[:, 2 * n:2 * n + 2, 0:O],
                                       ps[:, ROLL_BANKS[n], :].rearrange("p (t o) -> p t o", t=2),
                                       ACT.Copy).then_inc(h2_hi_ready, 1)
                    elif kind == "spread2":
                        act.wait_ge(row_done, T(3, 3))
                        for half in range(NH):
                            act.activation(alpha[:, nodes(half)], ps[:, ROW_A + half, :], ACT.Copy)\
                               .then_inc(rows_ready, 1)
                            act.activation(beta[:, nodes(half)], ps[:, ROW_B + half, :], ACT.Copy)\
                               .then_inc(rows_ready, 1)
                    elif kind == "weigh2":
                        if n == 0 and h == 0:
                            act.wait_ge(rows_ready, T(4, 0))
                            act.wait_ge(p1_summed, T(16, 16 * (0 if last_turn else 1)))
                        elif n == 0:
                            act.wait_ge(p2_ready, T(16, 8, -1))
                        if n >= 3:
                            act.wait_ge(p2_ready, T(16, 8 * h + n - 2, -1))
                        act.activation(p_full[:, n % 3, :], beta[:, nodes(h)], ACT.Identity,
                                       bias=slope_key[:, n:n + 1]).then_inc(p2_slope, 1)
                    elif kind == "split2":
                        act.wait_ge(p2_masked, T(16, 8 * h + n + 1, -1))
                        act.activation(p_full[:, n % 3, :], p_full[:, n % 3, :], ACT.Exp).then_inc(p2_full, 1)
                        act.wait_ge(p2_full, T(16, 8 * h + n + 1, -1))
                        if h == 1:
                            act.wait_ge(p2_used, T(16, n + 1, -1))
                        else:
                            act.wait_ge(p1_used, T(16, 0 if last_turn else 8 + n + 1))
                        act.activation(p_hi[:, n, :], p_full[:, n % 3, :], ACT.Copy).then_inc(p2_hi, 1)
                    elif kind == "normalise2":
                        act.wait_ge(part2_ready, T(8, 4 * h + n + 1, -1))
                        act.activation(e2[:, n % 2, :], ps[:, ATT2_BANKS[h][n], 0:O], ACT.Exp,
                                       scale=rsum2[:, n % 2:n % 2 + 1]).then_inc(e2_ready, 1)
                    elif kind == "clamp2":
                        act.wait_ge(att2_read, T(8, 4 * h + n + 1, -1))
                        act.activation(e2[:, n % 2, :], e2[:, n % 2, :], ACT.Exp, bias=neg_one[:]).then_inc(e2_done, 1)

            last_turn, first_turn = False, True
            run(FRONT, Turn(act, -1))
            run(whole(False, True), Turn(act, 0))
            first_turn = False
            with act.Fori(1, NB - 1) as b:
                run(whole(True, True), Turn(act, b))
            run(whole(True, False), Turn(act, NB - 1))
            last_turn = True
            run(LAST, Turn(act, NB))

        @block.vector
        def _(dve):
            dve.memset(ones[:], 1.0).then_inc(consts, 1)
            dve.memset(neg_one[:], -1.0).then_inc(consts, 1)
            dve.memset(p_sum[:], 0.0).then_inc(consts, 1)
            dve.memset(rsum2[:], 0.0).then_inc(consts, 1)
            dve.wait_ge(a_loaded, 48)
            dve.wait_ge(w_loaded, 96)
            for k in range(KH):
                for s in range(2):
                    if k + s:
                        dve.wait_ge(keys_set, 2 * k + s)
                    dve.tensor_tensor_reduce(out=a_junk, in0=wf_sb[:, k, :], in1=a_rows[:, s, :], scale=1.0,
                                             scalar=0.0, op0=ALU.mult, op1=ALU.add,
                                             accum_out=v1_sb[:, k, s:s + 1]).then_inc(keys_set, 1)
            for k in range(KO):
                for s in range(2):
                    dve.wait_ge(keys_set, 2 * KH + 2 * k + s)
                    dve.tensor_tensor_reduce(out=a_junk[:, 0:O], in0=wh_sb[:, k, :],
                                             in1=a2_rows[:, 0, s * O:(s + 1) * O], scale=1.0,
                                             scalar=0.0, op0=ALU.mult, op1=ALU.add,
                                             accum_out=v2_sb[:, k, s:s + 1]).then_inc(keys_set, 1)
            for t in range(NT):
                dve.wait_ge(adj_loaded[t % 2], 16 * (t // 2 + 1))
                if t >= 2:
                    dve.wait_ge(adj_turned, 2 * (t - 1))
                dve.tensor_scalar(adj_sb[:, t, :], stage[:, t % 2, :], 0.0, None, ALU.is_gt).then_inc(adj_seen, 1)
                dve.tensor_scalar(stage_f[:, t % 2, :], stage[:, t % 2, :], 0.0, None, ALU.is_gt).then_inc(adj_seen, 1)
                if t >= 1:
                    turned_tile = t - 1
                    for h in range(NH):
                        dve.wait_ge(adj_turned, 2 * turned_tile + h + 1)
                        dve.tensor_scalar(hidden[:, h * TH:(h + 1) * TH, block_of(turned_tile)],
                                          ps[:, 4 * (turned_tile % 2) + h, :].rearrange("p (j i) -> p j i", j=TH),
                                          0.5, None, ALU.is_lt).then_inc(adj_used, 1)
            for h in range(NH):
                dve.wait_ge(adj_turned, 2 * (NT - 1) + h + 1)
                dve.tensor_scalar(hidden[:, h * TH:(h + 1) * TH, block_of(NT - 1)],
                                  ps[:, 4 * ((NT - 1) % 2) + h, :].rearrange("p (j i) -> p j i", j=TH),
                                  0.5, None, ALU.is_lt).then_inc(adj_used, 1)

            def run(steps, T, link_base):
                links = 0

                def link(ins, alone=False):
                    nonlocal links
                    ins.then_inc(dve_link, 1)
                    links += 1
                    dve.wait_ge(dve_link, link_base + links)
                    if alone:
                        dve.sem_inc(waited_dve)

                for kind, h, n in steps:
                    if kind == "store_h":
                        dve.wait_ge(h_hi_ready, T(8, n + 1, 1))
                        dve.tensor_tensor(h_lo[:, n, :], ps[:, ROLL_BANKS[n % 4], :], h_hi[:, n, :].bitcast(F32),
                                          ALU.subtract).then_inc(h_ready, 1)
                    elif kind == "keys1":
                        dve.wait_ge(keys1_done, T(1, 1, 1))
                        link(dve.tensor_copy(keys1[:].rearrange("p t s -> p (t s)"), ps[:, KEY1_BANK, 0:2 * NT]))
                        dve.tensor_reduce(top1[:], keys1[:, :, 1], AX.X, ALU.max).then_inc(top1_ready, 1)
                    elif kind == "gap1":
                        dve.wait_ge(top1_shared, T(1, 1, 1))
                        dve.tensor_scalar(neg_top[:, 0:1], top1_all[:], -1.0, None, ALU.mult)
                        dve.tensor_scalar(neg_top[:, 1:2], top1_all[:], -SLOPE, None, ALU.mult)
                        dve.tensor_scalar(gap[:], keys1[:, :, 0], top1_all[:], RATIO_CAP, ALU.add, ALU.min)\
                           .then_inc(gap_ready, 1)
                    elif kind == "weigh1":
                        ahead = 1 - h
                        if h == 0 and n == 0:
                            dve.wait_ge(exp_ready, T(1, 1, 1))
                            dve.wait_ge(ratio_ready, T(2, 2, 1))
                        if n >= 3:
                            dve.wait_ge(p1_summed, T(16, 8 * h + n - 2, ahead))
                        elif h == 1:
                            dve.wait_ge(p1_summed, T(16, 8))
                        dve.tensor_scalar(p_full[:, n % 3, :], ratio[:, nodes(h)], key_exp[:, 0, n:n + 1],
                                          key_exp[:, 1, n:n + 1], ALU.mult, ALU.max).then_inc(p1_full, 1)
                    elif kind == "split1":
                        ahead = 1 - h
                        dve.wait_ge(p1_hi, T(16, 8 * h + n + 1, ahead))
                        dve.tensor_tensor(p_lo[:, n, :], p_full[:, n % 3, :], p_hi[:, n, :].bitcast(F32),
                                          ALU.subtract).then_inc(p1_ready, 1)
                        if n == 0:
                            before = T(2, h, ahead)
                            if not isinstance(before, int) or before > 0:
                                dve.wait_ge(sum1_done, before)
                            ins = dve.tensor_copy(p_sum[:], p_full[:, n % 3, :])
                        else:
                            dve.wait_ge(p1_summed, T(16, 8 * h + n, ahead))
                            ins = dve.tensor_tensor(p_sum[:], p_sum[:], p_full[:, n % 3, :], ALU.add)
                        ins.then_inc(p1_summed, 1)
                    elif kind == "sum1":
                        dve.wait_ge(sum1_done, T(2, h + 1))
                        dve.reciprocal(rsum1[:], ps[:, SUM_BANK[h], :]).then_inc(rsum_ready, 1)
                    elif kind == "normalise1":
                        if n >= 2 or h == 1:
                            dve.wait_ge(post_done, T(8, 4 * h + n - 1))
                        dve.wait_ge(rsum_ready, T(2, h + 1))
                        dve.wait_ge(p1_used, T(16, 8 * h + 8))
                        dve.tensor_tensor(u1[:, n % 2, :], ps[:, ATT1_BANKS[h][n], :], rsum1[:], ALU.mult)\
                           .then_inc(normed, 1)
                    elif kind == "clamp1":
                        dve.wait_ge(e1_ready, T(8, 4 * h + n + 1))
                        dve.tensor_scalar(e1[:, n % 2, :], e1[:, n % 2, :], 1.0, None, ALU.min).then_inc(clamped1, 1)
                    elif kind == "residual1":
                        dve.wait_ge(e1_done, T(8, 4 * h + n + 1))
                        link(dve.scalar_tensor_tensor(u1[:, n % 2, :], u1[:, n % 2, :], 0.0, e1[:, n % 2, :],
                                                      ALU.max, ALU.add))
                        dve.scalar_tensor_tensor(act1[:, n, nodes(h)], u1[:, n % 2, :], -1.0, act1[:, n, nodes(h)],
                                                 ALU.add, ALU.add).then_inc(post_done, 1)
                    elif kind == "store_h2":
                        dve.wait_ge(h2_hi_ready, T(4, n + 1))
                        dve.tensor_tensor(h2_lo[:, 2 * n:2 * n + 2, :],
                                          ps[:, ROLL_BANKS[n], :].rearrange("p (t o) -> p t o", t=2),
                                          h2_hi[:, 2 * n:2 * n + 2, 0:O].bitcast(F32),
                                          ALU.subtract).then_inc(h2_ready, 1)
                    elif kind == "keys2":
                        dve.wait_ge(keys2_done, T(1, 1))
                        dve.tensor_copy(keys2[:].rearrange("p t s -> p (t s)"), ps[:, KEY2_BANK, 0:2 * NT])\
                           .then_inc(keys2_read, 1)
                        dve.wait_ge(keys2_read, T(1, 1))
                        link(dve.tensor_scalar(neg_key[:], keys2[:, :, 1], -1.0, None, ALU.mult))
                        link(dve.tensor_scalar(slope_key[:], keys2[:, :, 1], SLOPE, None, ALU.mult))
                        dve.tensor_reduce(low2[:], neg_key[:], AX.X, ALU.max).then_inc(low2_ready, 1)
                        link(dve.tensor_scalar(best[:], keys2[:, :, 0], SLOPE, None, ALU.mult))
                    elif kind == "lift2":
                        dve.wait_ge(low2_shared, T(1, 1))
                        dve.tensor_scalar(lift[:], low2_all[:], 1.0, None, ALU.add)
                        dve.tensor_scalar(key_pos[:], keys2[:, :, 1], low2_all[:], 1.0, ALU.add, ALU.add)\
                           .then_inc(pos_ready, 1)
                    elif kind == "seen2":
                        if n == 0:
                            dve.wait_ge(row_done, T(3, 1))
                        else:
                            dve.wait_ge(seen_set, T(8, n))
                        dve.sem_inc(waited_dve)
                        dve.tensor_tensor_reduce(out=junk[:], in0=adj_sb[:, n, :],
                                                 in1=ps[:, ROW_B:ROW_B + 2, :].rearrange("p a b -> p (a b)"),
                                                 scale=1.0, scalar=0.0, op0=ALU.mult, op1=ALU.max,
                                                 accum_out=seen[:, n:n + 1]).then_inc(seen_set, 1)
                    elif kind == "rows2":
                        dve.wait_ge(seen_set, T(8, 8))
                        dve.tensor_scalar(lone[:], seen[:], 0.5, NEG_INF, ALU.is_lt, ALU.mult)
                        link(dve.tensor_scalar(best[:], seen[:], lift[:], None, ALU.subtract))
                        link(dve.tensor_tensor(best[:], best[:], keys2[:, :, 0], ALU.add))
                        link(dve.scalar_tensor_tensor(top2[:], best[:], SLOPE, best[:], ALU.mult, ALU.max))
                        link(dve.tensor_tensor(top2[:], top2[:], lone[:], ALU.add))
                        link(dve.tensor_tensor(alpha_col[:], keys2[:, :, 0], top2[:], ALU.subtract))
                        dve.scalar_tensor_tensor(beta_col[:], keys2[:, :, 0], SLOPE, top2[:], ALU.mult, ALU.subtract)\
                           .then_inc(cols_ready, 1)
                    elif kind == "weigh2":
                        if n == 0 and h == 0:
                            dve.wait_ge(rows_ready, T(4, 0))
                        dve.wait_ge(p2_slope, T(16, 8 * h + n + 1, -1))
                        link(dve.scalar_tensor_tensor(p_full[:, n % 3, :], alpha[:, nodes(h)], keys2[:, n, 1:2],
                                                      p_full[:, n % 3, :], ALU.add, ALU.max))
                        dve.scalar_tensor_tensor(p_full[:, n % 3, :], hidden[:, n, nodes(h)], NEG_INF,
                                                 p_full[:, n % 3, :], ALU.mult, ALU.add).then_inc(p2_masked, 1)
                    elif kind == "split2":
                        dve.wait_ge(p2_hi, T(16, 8 * h + n + 1, -1))
                        dve.tensor_tensor(p_lo[:, n, :], p_full[:, n % 3, :], p_hi[:, n, :].bitcast(F32),
                                          ALU.subtract).then_inc(p2_ready, 1)
                    elif kind == "normalise2":
                        bank = ps[:, ATT2_BANKS[h][n], :]
                        dve.wait_ge(p2_used, T(16, 8 * h + 8, -1))
                        link(dve.reciprocal(rsum2[:, n % 2:n % 2 + 1], bank[:, O:O + 1]))
                        dve.tensor_scalar(u2[:, n % 3, :], bank[:, 0:O], rsum2[:, n % 2:n % 2 + 1], 0.0,
                                          ALU.mult, ALU.max).then_inc(part2_ready, 1)
                    elif kind == "clamp2":
                        dve.wait_ge(e2_ready, T(8, 4 * h + n + 1, -1))
                        dve.tensor_scalar(e2[:, n % 2, :], e2[:, n % 2, :], 1.0, None, ALU.min).then_inc(att2_read, 1)
                    elif kind == "residual2":
                        u = u2[:, n % 3, :]
                        tile = h * TH + n
                        dve.wait_ge(e2_done, T(8, 4 * h + n + 1, -1))
                        link(dve.tensor_tensor(u, u, e2[:, n % 2, :], ALU.add))
                        link(dve.tensor_tensor(u, u, act2[:, tile, :], ALU.add))
                        dve.wait_ge(y_loaded[h], T(16, 0))
                        link(dve.scalar_tensor_tensor(y[:, h, n, :], u, 0.0, y[:, h, n, :], ALU.max, ALU.add))
                        link(dve.bn_stats(stats[:, n % 2, :], y[:, h, n, :]), alone=True)
                        dve.bn_aggr(moments[:, n, :], stats[:, n % 2, :]).then_inc(moments_ready, 1)
                    elif kind == "scale2":
                        dve.wait_ge(moments_ready, T(8, 4 * h + 4, -1))
                        dve.tensor_scalar(var_eps[:], moments[:, :, 1], LN_EPS, None, ALU.add).then_inc(var_ready, 1)
                        dve.wait_ge(rstd_ready, T(2, h + 1, -1))
                        for t in range(TH):
                            ins = dve.tensor_scalar(y[:, h, t, :], y[:, h, t, :], moments[:, t, 0:1],
                                                    rstd[:, t:t + 1], ALU.subtract, ALU.mult)
                        ins.then_inc(y_ready, 1)
                assert links == links_of(steps), (links, links_of(steps))

            dve.wait_ge(keys_set, 12)
            run(FRONT, Turn(dve, -1), 0)
            run(whole(False, True), Turn(dve, 0), LINKS_FRONT)
            base = LINKS_FRONT + LINKS_FIRST
            with dve.Fori(1, NB - 1) as b:
                T = Turn(dve, b)
                run(whole(True, True), T, T(LINKS, base, -1))
            run(whole(True, False), Turn(dve, NB - 1), base + (NB - 2) * LINKS)
            run(LAST, Turn(dve, NB), base + (NB - 2) * LINKS + links_of(whole(True, False)))


NAMES = ["x", "adj", "L0_gnn_mlp1_w", "L0_gnn_mlp1_b", "L0_gnn_mlp2_w", "L0_gnn_mlp2_b", "L0_gnn_W_fc",
         "L0_gnn_a_fc", "L0_gnn_W_hand", "L0_gnn_a_hand"]


def kernel(**inputs):
    import numpy as np
    import concourse.bacc as bacc
    from concourse.bass_utils import run_bass_kernel_spmd

    nc = bacc.Bacc("TRN2", target_bir_lowering=False, num_devices=1)
    arrays, args = {}, []
    for name in NAMES:
        a = np.ascontiguousarray(inputs[name])
        arrays[name + "_dram"] = a
        args.append(nc.dram_tensor(name + "_dram", a.shape, mybir.dt.from_np(a.dtype), kind="ExternalInput").ap())
    out = nc.dram_tensor("out_dram", inputs["x"].shape, F32, kind="ExternalOutput").ap()
    build(nc, *args, out)
    result = run_bass_kernel_spmd(nc, [arrays], core_ids=[0])
    return result.results[0]["out_dram"]
```

```python
from contextlib import ExitStack

import concourse.bass as bass
from concourse import mybir

F32 = mybir.dt.float32
F32R = mybir.dt.float32r
BF16 = mybir.dt.bfloat16
I32 = mybir.dt.int32
U8 = mybir.dt.uint8
ALU = mybir.AluOpType
ACT = mybir.ActivationFunctionType
AX = mybir.AxisListType
ALL_MAX = bass.bass_isa.ReduceOp.max

P = 128
BANK = 512
SLOPE = 0.2
NEG_INF = -9000000000000000.0
RATIO_CAP = 75.0
LN_EPS = 1e-5

ATT1_BANKS = ((0, 1, 2, 3), (4, 5, 6, 7))
SUM_BANK = (4, 0)
MLP2_BANKS = ((1, 2), (6, 7))
ATT2_BANKS = ((3, 0, 4, 5), (1, 2, 6, 7))
XT_BANKS = ((1, 2), (3, 0))
MLP1_BANKS = ((1, 2, 6, 7), (3, 0, 4, 5))
ROLL_BANKS = (3, 0, 4, 5)
KEY2_BANK, KEY1_BANK = 1, 2
ROW_A, ROW_B = 1, 6


ITEMS = 4
TILES = 8


def unit1(h, n, t):
    return [(t, "full1", h, n), (t + 0.8, "hi1", h, n), (t + 1.7, "lo1", h, n)]


def unit2(h, n, t):
    return [(t, "slope2", h, n), (t + 1.0, "top2", h, n), (t + 2.5, "exp2", h, n), (t + 3.3, "hi2", h, n),
            (t + 4.2, "lo2", h, n)]


def after1(h, n, t):
    return [(t, "norm1", h, n), (t + 0.8, "low1", h, n), (t + 1.6, "elu1", h, n), (t + 2.4, "elu_elu1", h, n),
            (t + 3.2, "add1", h, n)]


def after2(h, n, t):
    return [(t, "rsum2", h, n), (t + 0.4, "part2", h, n), (t + 1.5, "elu2", h, n), (t + 2.2, "elu_elu2", h, n),
            (t + 3.0, "add2", h, n)]


def layer_norm(h, t):
    return [(t, "var2", h, 0), (t + 2.0, "shift2", h, 0), (t + 2.5, "scale2", h, 0)]


def next_graph(t_xt, t_relu, t_keys, t_h):
    steps = [(t_xt[h] + 0.6 * k, "xt", h, k) for h in range(2) for k in range(2)]
    steps += [(t_relu + 1.8 * (ITEMS * h + f), "relu1", h, f) for h in range(2) for f in range(ITEMS)]
    steps += [(t_keys, "keys1", 0, 0), (t_keys + 2, "gap1", 0, 0), (t_keys + 2.5, "exp1", 0, 0),
              (t_h + 9.5, "ratio1", 0, 0)]
    steps += [(t_h + 3.5 * (n + 1) + (3.5 if n > 1 else 0), "hi_h", 0, n) for n in range(TILES)]
    steps += [(t_h + 3.5 * (n + 1) + (3.5 if n > 1 else 0) + 0.7, "lo_h", 0, n) for n in range(TILES)]
    for n in range(TILES):
        steps += unit1(0, n, t_h + 10.5 + 2.4 * n)
    return steps


def timetable(second, nxt):
    steps = [(6.5, "rsum1", 0, 0), (36.5, "rsum1", 1, 0)]
    for n in range(TILES):
        steps += unit1(1, n, 2.6 * n + 1.8)
    for n in range(ITEMS):
        steps += after1(0, n, 22.5 + 3.4 * n) + after1(1, n, 43.5 + 2.2 * n)
    steps += [(50.5 + 0.6 * n, "relu2", 0, n) for n in range(2)] + [(68.3 + 0.6 * n, "relu2", 1, n) for n in range(2)]
    steps += [(115.3 + 0.6 * n, "residual", 0, n) for n in range(ITEMS)]
    steps += [(95.3 + 1.8 * n, "hi_h2", 0, n) for n in range(ITEMS)]
    steps += [(96.0 + 1.8 * n, "lo_h2", 0, n) for n in range(ITEMS)]
    steps += [(103.8, "keys2", 0, 0), (106.8, "lift2", 0, 0), (141.0, "rows2", 0, 0), (153.0, "spread2", 0, 0)]
    steps += [(128.5 + 1.5 * n, "seen2", 0, n) for n in range(TILES)]
    if second:
        for n in range(TILES):
            steps += unit2(0, n, 20.8 + 2.6 * n) + unit2(1, n, 52.5 + 3.2 * n)
        for n in range(ITEMS):
            steps += after2(0, n, 60.6 + 4.5 * n) + after2(1, n, 93.3 + 2.4 * n)
        steps += layer_norm(0, 78.5) + layer_norm(1, 104.5)
    if nxt:
        steps += next_graph((61.0, 69.2), 70.5, 114.8, 117.0)
    return sorted(steps)


def front_table():
    return sorted(next_graph((0.0, 2.0), 4.0, 19.0, 20.0))


def last_table():
    steps = []
    for n in range(TILES):
        steps += unit2(0, n, 2.6 * n) + unit2(1, n, 26.0 + 2.6 * n)
    for n in range(ITEMS):
        steps += after2(0, n, 26.2 + 4.0 * n) + after2(1, n, 60.0 + 3.0 * n)
    return sorted(steps + layer_norm(0, 46.0) + layer_norm(1, 80.0))


LINKS = {"top2": 1, "add1": 1, "rsum2": 1, "add2": 4, "keys1": 1, "keys2": 3, "rows2": 5}


def links_of(steps):
    return sum(LINKS.get(kind, 0) for _, kind, _, _ in steps)


def build(nc, x, adj, w1, b1, w2, b2, wf, af, wh, ah, out):
    NB, N, FI = x.shape
    H = w1.shape[1]
    O = w2.shape[1]
    KI, KH, KO, NT = FI // P, H // P, O // P, N // P
    NH = N // BANK
    TH = NT // NH
    ONES = 2
    assert FI == O and NH == 2 and KH == 4 and KO == 2 and KI == 2 and NT == 8 and NB >= 3

    with ExitStack() as ctx:
        def sb(name, shape, dt):
            return ctx.enter_context(nc.sbuf_tensor(name, shape, dt))

        def sem(name):
            return ctx.enter_context(nc.semaphore(name))

        w1_sb = sb("w1_sb", [P, KI, H], F32)
        wf_sb = sb("wf_sb", [P, KH, H], F32)
        w2_sb = sb("w2_sb", [P, KH, O], F32)
        wh_sb = sb("wh_sb", [P, KO, O], F32)
        b1_sb = sb("b1_sb", [P, KH], F32)
        b2_sb = sb("b2_sb", [P, KO], F32)
        v1_sb = sb("v1_sb", [P, KH, 2], F32)
        v2_sb = sb("v2_sb", [P, KO, 2], F32)
        adj_sb = sb("adj_sb", [P, NT, N], U8)
        hidden = sb("hidden", [P, NT, N], U8)
        ident = sb("ident", [P, P], F32)
        neg_one = sb("neg_one", [P, 1], F32)
        ones = sb("ones", [P, P], F32)
        neg_half = sb("neg_half", [P, TH], F32)

        x_in = sb("x_in", [P, TH, FI], F32)
        x_t = sb("x_t", [P, KI, N], F32)
        act1 = sb("act1", [P, KH, N], F32)
        h_hi = sb("h_hi", [P, NT, H], F32R)
        h_lo = sb("h_lo", [P, NT, H], F32R)
        act2_t = sb("act2_t", [P, KO, N], F32)
        act2 = sb("act2", [P, NT, O], F32)
        h2_hi = sb("h2_hi", [P, NT, O + ONES], F32R)
        h2_lo = sb("h2_lo", [P, NT, O], F32R)
        y = sb("y", [P, NH, TH, O], F32)

        p_hi = sb("p_hi", [P, NT, BANK], F32R)
        p_lo = sb("p_lo", [P, NT, BANK], F32R)
        p_full = sb("p_full", [P, 3, BANK], F32)
        p_sum = sb("p_sum", [P, BANK], F32)
        rsum1 = sb("rsum1", [P, BANK], F32)
        ratio = sb("ratio", [P, N], F32)
        alpha = sb("alpha", [P, N], F32)
        beta = sb("beta", [P, N], F32)
        u1 = sb("u1", [P, 2, BANK], F32)
        e1 = sb("e1", [P, 2, BANK], F32)
        u2 = sb("u2", [P, 2, O], F32)
        e2 = sb("e2", [P, 2, O], F32)
        junk = sb("junk", [P, N], U8)

        keys1 = sb("keys1", [P, NT, 2], F32)
        keys2 = sb("keys2", [P, NT, 2], F32)
        top1 = sb("top1", [P, 1], F32)
        top1_all = sb("top1_all", [P, 1], F32)
        neg_top = sb("neg_top", [P, 2], F32)
        gap = sb("gap", [P, NT], F32)
        key_exp = sb("key_exp", [P, 2, NT], F32)
        neg_key = sb("neg_key", [P, NT], F32)
        low2 = sb("low2", [P, 1], F32)
        low2_all = sb("low2_all", [P, 1], F32)
        lift = sb("lift", [P, 1], F32)
        key_pos = sb("key_pos", [P, NT], F32)
        seen = sb("seen", [P, NT], F32)
        lone = sb("lone", [P, NT], F32)
        best = sb("best", [P, NT], F32)
        top2 = sb("top2", [P, NT], F32)
        alpha_col = sb("alpha_col", [P, NT], F32)
        beta_col = sb("beta_col", [P, NT], F32)
        slope_key = sb("slope_key", [P, NT], F32)
        rsum2 = sb("rsum2", [P, 2, 2], F32)
        stats = sb("stats", [P, 2, 6], F32)
        moments = sb("moments", [P, TH, 2], F32)
        var_eps = sb("var_eps", [P, TH], F32)
        rstd = sb("rstd", [P, TH], F32)
        shift = sb("shift", [P, TH], F32)

        ps = ctx.enter_context(nc.psum_tensor("ps", [P, 8, BANK], F32))

        w_loaded, a_loaded = sem("w_loaded"), sem("a_loaded")
        adj_loaded = [sem("adj_loaded0"), sem("adj_loaded1")]
        x_loaded = [sem("x_loaded0"), sem("x_loaded1")]
        y_loaded = [sem("y_loaded0"), sem("y_loaded1")]
        y_stored = [sem("y_stored0"), sem("y_stored1")]
        zeroed, consts, ident_set = sem("zeroed"), sem("consts"), sem("ident_set")
        a_used, keys_set, ones_set = sem("a_used"), sem("keys_set"), sem("ones_set")
        adj_seen, adj_turned, adj_used = sem("adj_seen"), sem("adj_turned"), sem("adj_used")
        xt_done, mlp1_done, keys1_done, h_done = sem("xt_done"), sem("mlp1_done"), sem("keys1_done"), sem("h_done")
        sum1_done, mlp2_done = sem("sum1_done"), sem("mlp2_done")
        res_done, h2_done, keys2_done = sem("res_done"), sem("h2_done"), sem("keys2_done")
        gap_spread, row_done = sem("gap_spread"), sem("row_done")
        p1_used, p2_used = sem("p1_used"), sem("p2_used")
        xt_ready, act1_ready = sem("xt_ready"), sem("act1_ready")
        h_hi_ready, h_ready = sem("h_hi_ready"), sem("h_ready")
        keys1_read, top1_ready, top1_shared = sem("keys1_read"), sem("top1_ready"), sem("top1_shared")
        gap_ready, exp_ready, ratio_ready = sem("gap_ready"), sem("exp_ready"), sem("ratio_ready")
        p1_full, p1_hi, p1_ready = sem("p1_full"), sem("p1_hi"), sem("p1_ready")
        waited_pool, waited_dve = sem("waited_pool"), sem("waited_dve")
        rsum_ready, p1_summed, seen_set = sem("rsum_ready"), sem("p1_summed"), sem("seen_set")
        normed, e1_low, e1_exp, e1_done, post_done = (
            sem("normed"), sem("e1_low"), sem("e1_exp"), sem("e1_done"), sem("post_done"))
        act2_ready, res_ready, h2_hi_ready, h2_ready = (
            sem("act2_ready"), sem("res_ready"), sem("h2_hi_ready"), sem("h2_ready"))
        keys2_read, low2_ready, low2_shared, pos_ready = (
            sem("keys2_read"), sem("low2_ready"), sem("low2_shared"), sem("pos_ready"))
        cols_ready, rows_ready = sem("cols_ready"), sem("rows_ready")
        p2_slope, p2_masked, p2_full, p2_hi, p2_ready = (
            sem("p2_slope"), sem("p2_masked"), sem("p2_full"), sem("p2_hi"), sem("p2_ready"))
        rsum2_ready, e2_low, e2_exp, att2_read, e2_done, moments_ready, shift_ready = (
            sem("rsum2_ready"), sem("e2_low"), sem("e2_exp"), sem("att2_read"), sem("e2_done"),
            sem("moments_ready"), sem("shift_ready"))
        var_ready, rstd_ready, y_ready, dve_link = (
            sem("var_ready"), sem("rstd_ready"), sem("y_ready"), sem("dve_link"))

        class Turn:

            def __init__(self, eng, b):
                self.eng, self.b, self.times = eng, b, {}

            def __call__(self, per, n, ahead=0):
                if isinstance(self.b, int):
                    return (self.b + ahead) * per + n
                if per not in self.times:
                    self.times[per] = self.eng.snap(self.b * per)
                return self.times[per] + (ahead * per + n)

        FRONT, FIRST, STEADY = front_table(), timetable(False, True), timetable(True, True)
        FINISH, LAST = timetable(True, False), last_table()

        def nodes(h):
            return slice(h * BANK, (h + 1) * BANK)

        def block_of(n):
            return slice(n * P, (n + 1) * P)

        x_v = x.rearrange("b (h t p) f -> b h p t f", p=P, t=TH)
        out_v = out.rearrange("b (h t p) f -> b h p t f", p=P, t=TH)
        stage = act1[:, 0:2, :].bitcast(I32)
        stage_f = act1[:, 2:4, :]
        a_rows = p_full[:, 0:2, :]
        a2_rows = u1[:, 0:1, :]
        a_junk = e1[:, 0, :]

        block = ctx.enter_context(nc.Block())

        @block.sync
        def _(sp):
            for dst, src in ((w1_sb, w1), (wf_sb, wf), (w2_sb, w2), (wh_sb, wh)):
                sp.dma_start(dst[:], src.rearrange("(k p) f -> p k f", p=P)).then_inc(w_loaded, 16)
            with nc.allow_non_contiguous_dma(reason="biases, a few hundred elements, once"):
                sp.dma_start(b1_sb[:], b1.rearrange("(k p) -> p k", p=P)).then_inc(w_loaded, 16)
                sp.dma_start(b2_sb[:], b2.rearrange("(k p) -> p k", p=P)).then_inc(w_loaded, 16)
            a_row = af.rearrange("(s f) c -> (c s) f", s=2)
            a2_row = ah.rearrange("(s f) c -> c (s f)", s=2)
            for s in range(2):
                sp.dma_start(a_rows[:, s, :], a_row[s:s + 1, :].to_broadcast([P, H])).then_inc(a_loaded, 16)
            sp.dma_start(a2_rows[:, 0, :], a2_row[0:1, :].to_broadcast([P, 2 * O])).then_inc(a_loaded, 16)
            for t in range(NT):
                if t >= 2:
                    sp.wait_ge(adj_seen, 2 * (t - 1))
                sp.dma_start(stage[:, t % 2, :], adj[t * P:(t + 1) * P, :]).then_inc(adj_loaded[t % 2], 16)

            def load_x(T, b, ahead):
                for h in range(NH):
                    n = T(4, 2 * h, ahead)
                    if not isinstance(n, int) or n > 0:
                        sp.wait_ge(xt_done, n)
                    sp.dma_start(x_in[:], x_v[b + ahead, h]).then_inc(x_loaded[h], 16)

            def pass_y(T, b, first):
                for h in range(NH):
                    if not first:
                        sp.wait_ge(y_stored[h], T(16, 0, -1))
                    sp.dma_start(y[:, h], x_v[b - 1, h]).then_inc(y_loaded[h], 16)

            def store_y(T, b, h):
                sp.wait_ge(y_ready, T(2, h + 1, -1))
                sp.dma_start(out_v[b - 1, h], y[:, h]).then_inc(y_stored[h], 16)

            def steady(b, first=False, nxt=True):
                T = Turn(sp, b)
                pass_y(T, b, first)
                store_half(T, b, nxt)

            def store_half(T, b, nxt):
                if nxt:
                    for h in range(NH):
                        sp.wait_ge(xt_done, T(4, 2 * h, 1))
                        sp.dma_start(x_in[:], x_v[b + 1, h]).then_inc(x_loaded[h], 16)
                for h in range(NH):
                    store_y(T, b, h)

            load_x(Turn(sp, 0), 0, 0)
            load_x(Turn(sp, 0), 0, 1)
            steady(1, first=True)
            with sp.Fori(2, NB - 1) as b:
                steady(b)
            steady(NB - 1, nxt=False)
            steady(NB, nxt=False)
            for h in range(NH):
                sp.wait_ge(y_stored[h], 16 * NB)

        @block.gpsimd
        def _(pool):
            pool.memset(ident[:], 0.0).then_inc(zeroed, 1)
            pool.wait_ge(zeroed, 1)
            pool.affine_select(out=ident[:], in_=ident[:], compare_op=ALU.not_equal, fill=1.0, base=0,
                               pattern=[[-1, P]], channel_multiplier=1).then_inc(ident_set, 1)
            pool.memset(neg_half[:], -0.5).then_inc(zeroed, 1)
            pool.wait_ge(zeroed, 2)

            def top(T, ahead):
                pool.wait_ge(top1_ready, T(1, 1, ahead))
                pool.sem_inc(waited_pool)
                pool.partition_all_reduce(top1_all[:], top1[:], P, ALL_MAX).then_inc(top1_shared, 1)

            def low(T):
                pool.wait_ge(low2_ready, T(1, 1))
                pool.sem_inc(waited_pool)
                pool.partition_all_reduce(low2_all[:], low2[:], P, ALL_MAX).then_inc(low2_shared, 1)

            def deviation(T, h):
                pool.wait_ge(var_ready, T(2, h + 1, -1))
                pool.tensor_tensor(rstd[:], var_eps[:], neg_half[:], ALU.pow).then_inc(rstd_ready, 1)

            def iteration(b, second=True, nxt=True):
                T = Turn(pool, b)
                if second:
                    deviation(T, 0)
                    deviation(T, 1)
                low(T)
                if nxt:
                    top(T, 1)

            top(Turn(pool, 0), 0)
            iteration(0, second=False)
            with pool.Fori(1, NB - 1) as b:
                iteration(b)
            iteration(NB - 1, nxt=False)
            T = Turn(pool, NB)
            deviation(T, 0)
            deviation(T, 1)

        @block.tensor
        def _(pe):
            def turn_x(T, ahead, h):
                pe.wait_ge(x_loaded[h], T(16, 16, ahead))
                for k in range(KI):
                    for t in range(TH):
                        last = pe.transpose(ps[:, XT_BANKS[h][k], block_of(t)], x_in[:, t, block_of(k)], ident[:])
                    last.then_inc(xt_done, 1)

            def mlp1(T, ahead, h):
                pe.wait_ge(xt_ready, T(4, 2 * h + 2, ahead))
                for f in range(KH):
                    for k in range(KI):
                        last = pe.matmul(ps[:, MLP1_BANKS[h][f], :], w1_sb[:, k, block_of(f)], x_t[:, k, nodes(h)],
                                         start=(k == 0), stop=(k == KI - 1))
                    last.then_inc(mlp1_done, 1)

            def keys(src, v, n, bank, done):
                for t in range(NT):
                    for k in range(n):
                        last = pe.matmul(ps[:, bank, 2 * t:2 * t + 2], src[:, k, block_of(t)], v[:, k, :],
                                         start=(k == 0), stop=(k == n - 1))
                last.then_inc(done, 1)

            def spread(col, bank, done):
                for t in range(NT):
                    last = pe.matmul(ps[:, bank + t // TH, block_of(t % TH)], col[:, t:t + 1].to_broadcast([P, P]),
                                     ident[:], start=True, stop=True)
                last.then_inc(done, 1)

            def h_tile(T, ahead, t):
                if t >= len(ROLL_BANKS):
                    pe.wait_ge(h_ready, T(8, t - 3, ahead))
                for k in range(KH):
                    last = pe.matmul(ps[:, ROLL_BANKS[t % 4], :], act1[:, k, block_of(t)], wf_sb[:, k, :],
                                     start=(k == 0), stop=(k == KH - 1))
                last.then_inc(h_done, 1)

            def attend1(T, h):
                for j in range(NT):
                    if j == 2 + 3 * h:
                        pe.wait_ge(p1_summed, T(16, 8 * h + 8))
                        if h == 1:
                            pe.wait_ge(normed, T(8, 1))
                        pe.matmul(ps[:, SUM_BANK[h], :], ones[:], p_sum[:], start=True, stop=True).then_inc(sum1_done, 1)
                    if h == 1 and j == 0:
                        pe.wait_ge(rsum_ready, T(2, 1))
                    pe.wait_ge(p1_ready, T(16, 8 * h + j + 1))
                    for f in range(KH):
                        acc = ps[:, ATT1_BANKS[h][f], :]
                        pe.matmul(acc, h_hi[:, j, block_of(f)], p_hi[:, j, :], start=(j == 0), stop=False)
                        pe.matmul(acc, h_hi[:, j, block_of(f)], p_lo[:, j, :], start=False, stop=False)
                        last = pe.matmul(acc, h_lo[:, j, block_of(f)], p_hi[:, j, :], start=False, stop=(j == NT - 1))
                    last.then_inc(p1_used, 1)

            def attend2(T, h):
                for j in range(NT):
                    pe.wait_ge(p2_ready, T(16, 8 * h + j + 1, -1))
                    for q in range(TH):
                        acc = ps[:, ATT2_BANKS[h][q], 0:O + ONES]
                        pe.matmul(acc, p_hi[:, j, block_of(q)], h2_hi[:, j, :], start=(j == 0), stop=False)
                        pe.matmul(acc, p_lo[:, j, block_of(q)], h2_hi[:, j, :], start=False, stop=False)
                        last = pe.matmul(ps[:, ATT2_BANKS[h][q], 0:O], p_hi[:, j, block_of(q)], h2_lo[:, j, :],
                                         start=False, stop=(j == NT - 1))
                    last.then_inc(p2_used, 1)

            def mlp2(T, h):
                pe.wait_ge(post_done, T(8, 4 * h + 4))
                for o in range(KO):
                    for k in range(KH):
                        last = pe.matmul(ps[:, MLP2_BANKS[h][o], :], w2_sb[:, k, block_of(o)], act1[:, k, nodes(h)],
                                         start=(k == 0), stop=(k == KH - 1))
                    last.then_inc(mlp2_done, 1)

            def iteration(b, second=True, nxt=True):
                T = Turn(pe, b)
                pe.wait_ge(h_ready, T(8, 8))
                if second:
                    pe.wait_ge(rows_ready, T(4, 4, -1))
                pe.wait_ge(ratio_ready, T(2, 2))
                attend1(T, 0)
                attend1(T, 1)
                mlp2(T, 0)
                if second:
                    pe.wait_ge(h2_ready, T(4, 4, -1))
                    pe.wait_ge(rsum_ready, T(2, 2))
                    pe.wait_ge(normed, T(8, 6))
                    attend2(T, 0)
                if nxt:
                    pe.wait_ge(act2_ready, T(4, 2))
                    turn_x(T, 1, 0)
                mlp2(T, 1)
                if nxt:
                    if second:
                        pe.wait_ge(att2_read, T(8, 2, -1))
                    else:
                        pe.wait_ge(rsum_ready, T(2, 2))
                    turn_x(T, 1, 1)
                pe.wait_ge(act2_ready, T(4, 4))
                if nxt:
                    mlp1(T, 1, 0)
                    if second:
                        pe.wait_ge(att2_read, T(8, 4, -1))
                    mlp1(T, 1, 1)
                if second:
                    if nxt:
                        pe.wait_ge(act1_ready, T(8, 4, 1))
                    attend2(T, 1)
                if nxt:
                    pe.wait_ge(act1_ready, T(8, 8, 1))
                elif second:
                    pe.wait_ge(att2_read, T(8, 4, -1))
                for n in range(4):
                    for t in (2 * n, 2 * n + 1):
                        for k in range(KO):
                            last = pe.matmul(ps[:, ROLL_BANKS[n], (t % 2) * O:(t % 2 + 1) * O],
                                             act2_t[:, k, block_of(t)], wh_sb[:, k, :],
                                             start=(k == 0), stop=(k == KO - 1))
                    last.then_inc(h2_done, 1)
                if second:
                    pe.wait_ge(att2_read, T(8, 6, -1))
                keys(act2_t, v2_sb, KO, KEY2_BANK, keys2_done)
                if nxt:
                    keys(act1, v1_sb, KH, KEY1_BANK, keys1_done)
                for n in range(4):
                    pe.wait_ge(h2_ready, T(4, n + 1))
                    for t in (2 * n, 2 * n + 1):
                        for o in range(KO):
                            at = (t % 2) * O + o * P
                            last = pe.transpose(ps[:, ROLL_BANKS[n], at:at + P], act2_t[:, o, block_of(t)], ident[:])
                    last.then_inc(res_done, 1)
                if nxt:
                    for t in range(2):
                        pe.wait_ge(res_ready, T(4, t + 1))
                        h_tile(T, 1, t)
                    pe.wait_ge(gap_ready, T(1, 1, 1))
                    pe.wait_ge(keys2_read, T(1, 1))
                    spread(gap, ROW_A, gap_spread)
                if second:
                    pe.wait_ge(att2_read, T(8, 8, -1))
                pe.wait_ge(pos_ready, T(1, 1))
                spread(key_pos, ROW_B, row_done)
                if nxt:
                    for t in range(2, NT):
                        if t < 4:
                            pe.wait_ge(res_ready, T(4, t + 1))
                        h_tile(T, 1, t)
                    pe.wait_ge(ratio_ready, T(2, 2, 1))
                pe.wait_ge(cols_ready, T(1, 1))
                spread(alpha_col, ROW_A, row_done)
                spread(beta_col, ROW_B, row_done)

            pe.wait_ge(ident_set, 1)
            pe.wait_ge(consts, 4)
            for t in range(NT):
                pe.wait_ge(adj_seen, 2 * (t + 1))
                for h in range(NH):
                    if t >= 2:
                        pe.wait_ge(adj_used, 2 * (t - 1) + h - 1)
                    for j in range(TH):
                        last = pe.transpose(ps[:, 4 * (t % 2) + h, block_of(j)],
                                            stage_f[:, t % 2, block_of(h * TH + j)], ident[:])
                    last.then_inc(adj_turned, 1)
            pe.wait_ge(w_loaded, 96)
            pe.wait_ge(keys_set, 12)
            pe.wait_ge(adj_used, 16)
            T = Turn(pe, 0)
            turn_x(T, 0, 0)
            turn_x(T, 0, 1)
            mlp1(T, 0, 0)
            pe.wait_ge(xt_ready, 4)
            mlp1(T, 0, 1)
            pe.wait_ge(act1_ready, 8)
            keys(act1, v1_sb, KH, KEY1_BANK, keys1_done)
            h_tile(T, 0, 0)
            h_tile(T, 0, 1)
            pe.wait_ge(gap_ready, 1)
            spread(gap, ROW_A, gap_spread)
            for t in range(2, NT):
                h_tile(T, 0, t)

            iteration(0, second=False)
            with pe.Fori(1, NB - 1) as b:
                iteration(b)
            iteration(NB - 1, nxt=False)
            T = Turn(pe, NB)
            pe.wait_ge(rows_ready, 4 * NB)
            pe.wait_ge(h2_ready, 4 * NB)
            attend2(T, 0)
            attend2(T, 1)

        @block.scalar
        def _(act):
            act.wait_ge(consts, 4)
            for t in range(NT):
                act.activation(h2_hi[:, t, O:O + ONES], ones[:, 0:ONES], ACT.Copy).then_inc(ones_set, 1)
            act.wait_ge(w_loaded, 96)

            def run(steps, T):
                for _, kind, h, n in steps:
                    if kind == "xt":
                        act.wait_ge(xt_done, T(4, 2 * h + n + 1, 1))
                        act.activation(x_t[:, n, nodes(h)], ps[:, XT_BANKS[h][n], :], ACT.Copy).then_inc(xt_ready, 1)
                    elif kind == "relu1":
                        act.wait_ge(mlp1_done, T(8, 4 * h + n + 1, 1))
                        act.activation(act1[:, n, nodes(h)], ps[:, MLP1_BANKS[h][n], :], ACT.Relu,
                                       bias=b1_sb[:, n:n + 1]).then_inc(act1_ready, 1)
                    elif kind == "hi_h":
                        act.wait_ge(h_done, T(8, n + 1, 1))
                        act.activation(h_hi[:, n, :], ps[:, ROLL_BANKS[n % 4], :], ACT.Copy).then_inc(h_hi_ready, 1)
                    elif kind == "exp1":
                        act.wait_ge(gap_ready, T(1, 1, 1))
                        act.activation(key_exp[:, 0, :], keys1[:, :, 1], ACT.Exp, bias=neg_top[:, 0:1])
                        act.activation(key_exp[:, 1, :], keys1[:, :, 1], ACT.Exp, bias=neg_top[:, 1:2],
                                       scale=SLOPE).then_inc(exp_ready, 1)
                    elif kind == "ratio1":
                        act.wait_ge(gap_spread, T(1, 1, 1))
                        for half in range(NH):
                            act.activation(ratio[:, nodes(half)], ps[:, ROW_A + half, :], ACT.Exp,
                                           scale=1.0 - SLOPE).then_inc(ratio_ready, 1)
                    elif kind == "hi1":
                        act.wait_ge(p1_full, T(16, 8 * h + n + 1, 1 - h))
                        if h == 1:
                            act.wait_ge(p1_used, T(16, n + 1))
                        act.activation(p_hi[:, n, :], p_full[:, n % 3, :], ACT.Copy).then_inc(p1_hi, 1)
                    elif kind == "low1":
                        act.wait_ge(normed, T(8, 4 * h + n + 1))
                        act.activation(e1[:, n % 2, :], u1[:, n % 2, :], ACT.Relu, scale=-1.0).then_inc(e1_low, 1)
                    elif kind == "elu1":
                        act.wait_ge(e1_low, T(8, 4 * h + n + 1))
                        act.activation(e1[:, n % 2, :], e1[:, n % 2, :], ACT.Exp, scale=-1.0).then_inc(e1_exp, 1)
                    elif kind == "elu_elu1":
                        act.wait_ge(e1_exp, T(8, 4 * h + n + 1))
                        act.activation(e1[:, n % 2, :], e1[:, n % 2, :], ACT.Exp, bias=neg_one[:]).then_inc(e1_done, 1)
                    elif kind == "relu2":
                        act.wait_ge(mlp2_done, T(4, 2 * h + n + 1))
                        act.activation(act2_t[:, n, nodes(h)], ps[:, MLP2_BANKS[h][n], :], ACT.Relu,
                                       bias=b2_sb[:, n:n + 1]).then_inc(act2_ready, 1)
                    elif kind == "residual":
                        act.wait_ge(res_done, T(4, n + 1))
                        if n == 0 and not first_turn:
                            act.wait_ge(moments_ready, T(8, 8, -1))
                        act.activation(act2[:, 2 * n:2 * n + 2, :],
                                       ps[:, ROLL_BANKS[n], :].rearrange("p (t o) -> p t o", t=2),
                                       ACT.Identity, bias=neg_one[:]).then_inc(res_ready, 1)
                    elif kind == "hi_h2":
                        act.wait_ge(h2_done, T(4, n + 1))
                        act.activation(h2_hi[:, 2 * n:2 * n + 2, 0:O],
                                       ps[:, ROLL_BANKS[n], :].rearrange("p (t o) -> p t o", t=2),
                                       ACT.Copy).then_inc(h2_hi_ready, 1)
                    elif kind == "spread2":
                        act.wait_ge(row_done, T(3, 3))
                        for half in range(NH):
                            act.activation(alpha[:, nodes(half)], ps[:, ROW_A + half, :], ACT.Copy)\
                               .then_inc(rows_ready, 1)
                            act.activation(beta[:, nodes(half)], ps[:, ROW_B + half, :], ACT.Copy)\
                               .then_inc(rows_ready, 1)
                    elif kind == "slope2":
                        if n == 0 and h == 0:
                            act.wait_ge(rows_ready, T(4, 0))
                            act.wait_ge(p1_summed, T(16, 16 * (0 if last_turn else 1)))
                        elif n == 0:
                            act.wait_ge(p2_ready, T(16, 8, -1))
                        if n >= 3:
                            act.wait_ge(p2_ready, T(16, 8 * h + n - 2, -1))
                        act.activation(p_full[:, n % 3, :], beta[:, nodes(h)], ACT.Identity,
                                       bias=slope_key[:, n:n + 1]).then_inc(p2_slope, 1)
                    elif kind == "exp2":
                        act.wait_ge(p2_masked, T(16, 8 * h + n + 1, -1))
                        act.activation(p_full[:, n % 3, :], p_full[:, n % 3, :], ACT.Exp).then_inc(p2_full, 1)
                    elif kind == "hi2":
                        act.wait_ge(p2_full, T(16, 8 * h + n + 1, -1))
                        if h == 1:
                            act.wait_ge(p2_used, T(16, n + 1, -1))
                        else:
                            act.wait_ge(p1_used, T(16, 0 if last_turn else 8 + n + 1))
                        act.activation(p_hi[:, n, :], p_full[:, n % 3, :], ACT.Copy).then_inc(p2_hi, 1)
                    elif kind == "part2":
                        act.wait_ge(rsum2_ready, T(8, 4 * h + n + 1, -1))
                        act.activation(e2[:, n % 2, :], ps[:, ATT2_BANKS[h][n], 0:O], ACT.Relu,
                                       scale=rsum2[:, n % 2, 1:2]).then_inc(e2_low, 1)
                        act.activation(u2[:, n % 2, :], ps[:, ATT2_BANKS[h][n], 0:O], ACT.Relu,
                                       scale=rsum2[:, n % 2, 0:1]).then_inc(att2_read, 1)
                    elif kind == "elu2":
                        act.wait_ge(e2_low, T(8, 4 * h + n + 1, -1))
                        act.activation(e2[:, n % 2, :], e2[:, n % 2, :], ACT.Exp, scale=-1.0).then_inc(e2_exp, 1)
                    elif kind == "elu_elu2":
                        act.wait_ge(e2_exp, T(8, 4 * h + n + 1, -1))
                        act.activation(e2[:, n % 2, :], e2[:, n % 2, :], ACT.Exp, bias=neg_one[:]).then_inc(e2_done, 1)
                    elif kind == "scale2":
                        act.wait_ge(shift_ready, T(2, h + 1, -1))
                        for t in range(TH):
                            ins = act.activation(y[:, h, t, :], y[:, h, t, :], ACT.Identity,
                                                 bias=shift[:, t:t + 1], scale=rstd[:, t:t + 1])
                        ins.then_inc(y_ready, 1)

            last_turn, first_turn = False, True
            run(FRONT, Turn(act, -1))
            run(FIRST, Turn(act, 0))
            first_turn = False
            with act.Fori(1, NB - 1) as b:
                run(STEADY, Turn(act, b))
            run(FINISH, Turn(act, NB - 1))
            last_turn = True
            run(LAST, Turn(act, NB))

        @block.vector
        def _(dve):
            dve.memset(ones[:], 1.0).then_inc(consts, 1)
            dve.memset(neg_one[:], -1.0).then_inc(consts, 1)
            dve.memset(p_sum[:], 0.0).then_inc(consts, 1)
            dve.memset(rsum2[:], 0.0).then_inc(consts, 1)
            dve.wait_ge(a_loaded, 48)
            dve.wait_ge(w_loaded, 96)
            for k in range(KH):
                for s in range(2):
                    if k + s:
                        dve.wait_ge(keys_set, 2 * k + s)
                    dve.tensor_tensor_reduce(out=a_junk, in0=wf_sb[:, k, :], in1=a_rows[:, s, :], scale=1.0,
                                             scalar=0.0, op0=ALU.mult, op1=ALU.add,
                                             accum_out=v1_sb[:, k, s:s + 1]).then_inc(keys_set, 1)
            for k in range(KO):
                for s in range(2):
                    dve.wait_ge(keys_set, 2 * KH + 2 * k + s)
                    dve.tensor_tensor_reduce(out=a_junk[:, 0:O], in0=wh_sb[:, k, :],
                                             in1=a2_rows[:, 0, s * O:(s + 1) * O], scale=1.0,
                                             scalar=0.0, op0=ALU.mult, op1=ALU.add,
                                             accum_out=v2_sb[:, k, s:s + 1]).then_inc(keys_set, 1)
            for t in range(NT):
                dve.wait_ge(adj_loaded[t % 2], 16 * (t // 2 + 1))
                if t >= 2:
                    dve.wait_ge(adj_turned, 2 * (t - 1))
                dve.tensor_scalar(adj_sb[:, t, :], stage[:, t % 2, :], 0.0, None, ALU.is_gt).then_inc(adj_seen, 1)
                dve.tensor_scalar(stage_f[:, t % 2, :], stage[:, t % 2, :], 0.0, None, ALU.is_gt).then_inc(adj_seen, 1)
                if t >= 1:
                    turned_tile = t - 1
                    for h in range(NH):
                        dve.wait_ge(adj_turned, 2 * turned_tile + h + 1)
                        dve.tensor_scalar(hidden[:, h * TH:(h + 1) * TH, block_of(turned_tile)],
                                          ps[:, 4 * (turned_tile % 2) + h, :].rearrange("p (j i) -> p j i", j=TH),
                                          0.5, None, ALU.is_lt).then_inc(adj_used, 1)
            for h in range(NH):
                dve.wait_ge(adj_turned, 2 * (NT - 1) + h + 1)
                dve.tensor_scalar(hidden[:, h * TH:(h + 1) * TH, block_of(NT - 1)],
                                  ps[:, 4 * ((NT - 1) % 2) + h, :].rearrange("p (j i) -> p j i", j=TH),
                                  0.5, None, ALU.is_lt).then_inc(adj_used, 1)

            def run(steps, T, link_base):
                links = 0

                def link(ins, alone=False):
                    nonlocal links
                    ins.then_inc(dve_link, 1)
                    links += 1
                    dve.wait_ge(dve_link, link_base + links)
                    if alone:
                        dve.sem_inc(waited_dve)

                for _, kind, h, n in steps:
                    if kind == "lo_h":
                        dve.wait_ge(h_hi_ready, T(8, n + 1, 1))
                        dve.tensor_tensor(h_lo[:, n, :], ps[:, ROLL_BANKS[n % 4], :], h_hi[:, n, :].bitcast(F32),
                                          ALU.subtract).then_inc(h_ready, 1)
                    elif kind == "keys1":
                        dve.wait_ge(keys1_done, T(1, 1, 1))
                        link(dve.tensor_copy(keys1[:].rearrange("p t s -> p (t s)"), ps[:, KEY1_BANK, 0:2 * NT]))
                        dve.tensor_reduce(top1[:], keys1[:, :, 1], AX.X, ALU.max).then_inc(top1_ready, 1)
                    elif kind == "gap1":
                        dve.wait_ge(top1_shared, T(1, 1, 1))
                        dve.tensor_scalar(neg_top[:, 0:1], top1_all[:], -1.0, None, ALU.mult)
                        dve.tensor_scalar(neg_top[:, 1:2], top1_all[:], -SLOPE, None, ALU.mult)
                        dve.tensor_scalar(gap[:], keys1[:, :, 0], top1_all[:], RATIO_CAP, ALU.add, ALU.min)\
                           .then_inc(gap_ready, 1)
                    elif kind == "full1":
                        ahead = 1 - h
                        if h == 0 and n == 0:
                            dve.wait_ge(exp_ready, T(1, 1, 1))
                            dve.wait_ge(ratio_ready, T(2, 2, 1))
                        if n >= 3:
                            dve.wait_ge(p1_summed, T(16, 8 * h + n - 2, ahead))
                        elif h == 1:
                            dve.wait_ge(p1_summed, T(16, 8))
                        dve.tensor_scalar(p_full[:, n % 3, :], ratio[:, nodes(h)], key_exp[:, 0, n:n + 1],
                                          key_exp[:, 1, n:n + 1], ALU.mult, ALU.max).then_inc(p1_full, 1)
                    elif kind == "lo1":
                        ahead = 1 - h
                        dve.wait_ge(p1_hi, T(16, 8 * h + n + 1, ahead))
                        dve.tensor_tensor(p_lo[:, n, :], p_full[:, n % 3, :], p_hi[:, n, :].bitcast(F32),
                                          ALU.subtract).then_inc(p1_ready, 1)
                        if n == 0:
                            before = T(2, h, ahead)
                            if not isinstance(before, int) or before > 0:
                                dve.wait_ge(sum1_done, before)
                            ins = dve.tensor_copy(p_sum[:], p_full[:, n % 3, :])
                        else:
                            dve.wait_ge(p1_summed, T(16, 8 * h + n, ahead))
                            ins = dve.tensor_tensor(p_sum[:], p_sum[:], p_full[:, n % 3, :], ALU.add)
                        ins.then_inc(p1_summed, 1)
                    elif kind == "rsum1":
                        dve.wait_ge(sum1_done, T(2, h + 1))
                        dve.reciprocal(rsum1[:], ps[:, SUM_BANK[h], :]).then_inc(rsum_ready, 1)
                    elif kind == "norm1":
                        if n >= 2 or h == 1:
                            dve.wait_ge(post_done, T(8, 4 * h + n - 1))
                        dve.wait_ge(rsum_ready, T(2, h + 1))
                        dve.wait_ge(p1_used, T(16, 8 * h + 8))
                        dve.tensor_tensor(u1[:, n % 2, :], ps[:, ATT1_BANKS[h][n], :], rsum1[:], ALU.mult)\
                           .then_inc(normed, 1)
                    elif kind == "add1":
                        dve.wait_ge(e1_done, T(8, 4 * h + n + 1))
                        link(dve.scalar_tensor_tensor(u1[:, n % 2, :], u1[:, n % 2, :], 0.0, e1[:, n % 2, :],
                                                      ALU.max, ALU.add))
                        dve.scalar_tensor_tensor(act1[:, n, nodes(h)], u1[:, n % 2, :], -1.0, act1[:, n, nodes(h)],
                                                 ALU.add, ALU.add).then_inc(post_done, 1)
                    elif kind == "lo_h2":
                        dve.wait_ge(h2_hi_ready, T(4, n + 1))
                        dve.tensor_tensor(h2_lo[:, 2 * n:2 * n + 2, :],
                                          ps[:, ROLL_BANKS[n], :].rearrange("p (t o) -> p t o", t=2),
                                          h2_hi[:, 2 * n:2 * n + 2, 0:O].bitcast(F32),
                                          ALU.subtract).then_inc(h2_ready, 1)
                    elif kind == "keys2":
                        dve.wait_ge(keys2_done, T(1, 1))
                        dve.tensor_copy(keys2[:].rearrange("p t s -> p (t s)"), ps[:, KEY2_BANK, 0:2 * NT])\
                           .then_inc(keys2_read, 1)
                        dve.wait_ge(keys2_read, T(1, 1))
                        link(dve.tensor_scalar(neg_key[:], keys2[:, :, 1], -1.0, None, ALU.mult))
                        link(dve.tensor_scalar(slope_key[:], keys2[:, :, 1], SLOPE, None, ALU.mult))
                        dve.tensor_reduce(low2[:], neg_key[:], AX.X, ALU.max).then_inc(low2_ready, 1)
                        link(dve.tensor_scalar(best[:], keys2[:, :, 0], SLOPE, None, ALU.mult))
                    elif kind == "lift2":
                        dve.wait_ge(low2_shared, T(1, 1))
                        dve.tensor_scalar(lift[:], low2_all[:], 1.0, None, ALU.add)
                        dve.tensor_scalar(key_pos[:], keys2[:, :, 1], low2_all[:], 1.0, ALU.add, ALU.add)\
                           .then_inc(pos_ready, 1)
                    elif kind == "seen2":
                        if n == 0:
                            dve.wait_ge(row_done, T(3, 1))
                        else:
                            dve.wait_ge(seen_set, T(8, n))
                        dve.sem_inc(waited_dve)
                        dve.tensor_tensor_reduce(out=junk[:], in0=adj_sb[:, n, :],
                                                 in1=ps[:, ROW_B:ROW_B + 2, :].rearrange("p a b -> p (a b)"),
                                                 scale=1.0, scalar=0.0, op0=ALU.mult, op1=ALU.max,
                                                 accum_out=seen[:, n:n + 1]).then_inc(seen_set, 1)
                    elif kind == "rows2":
                        dve.wait_ge(seen_set, T(8, 8))
                        dve.tensor_scalar(lone[:], seen[:], 0.5, NEG_INF, ALU.is_lt, ALU.mult)
                        link(dve.tensor_scalar(best[:], seen[:], lift[:], None, ALU.subtract))
                        link(dve.tensor_tensor(best[:], best[:], keys2[:, :, 0], ALU.add))
                        link(dve.scalar_tensor_tensor(top2[:], best[:], SLOPE, best[:], ALU.mult, ALU.max))
                        link(dve.tensor_tensor(top2[:], top2[:], lone[:], ALU.add))
                        link(dve.tensor_tensor(alpha_col[:], keys2[:, :, 0], top2[:], ALU.subtract))
                        dve.scalar_tensor_tensor(beta_col[:], keys2[:, :, 0], SLOPE, top2[:], ALU.mult, ALU.subtract)\
                           .then_inc(cols_ready, 1)
                    elif kind == "top2":
                        if n == 0 and h == 0:
                            dve.wait_ge(rows_ready, T(4, 0))
                        dve.wait_ge(p2_slope, T(16, 8 * h + n + 1, -1))
                        link(dve.scalar_tensor_tensor(p_full[:, n % 3, :], alpha[:, nodes(h)], keys2[:, n, 1:2],
                                                      p_full[:, n % 3, :], ALU.add, ALU.max))
                        dve.scalar_tensor_tensor(p_full[:, n % 3, :], hidden[:, n, nodes(h)], NEG_INF,
                                                 p_full[:, n % 3, :], ALU.mult, ALU.add).then_inc(p2_masked, 1)
                    elif kind == "lo2":
                        dve.wait_ge(p2_hi, T(16, 8 * h + n + 1, -1))
                        dve.tensor_tensor(p_lo[:, n, :], p_full[:, n % 3, :], p_hi[:, n, :].bitcast(F32),
                                          ALU.subtract).then_inc(p2_ready, 1)
                    elif kind == "rsum2":
                        dve.wait_ge(p2_used, T(16, 8 * h + 8, -1))
                        if n >= 2 or h == 1:
                            dve.wait_ge(att2_read, T(8, 4 * h + n - 1, -1))
                        link(dve.reciprocal(rsum2[:, n % 2, 0:1], ps[:, ATT2_BANKS[h][n], O:O + 1]))
                        dve.tensor_scalar(rsum2[:, n % 2, 1:2], rsum2[:, n % 2, 0:1], -1.0, None, ALU.mult)\
                           .then_inc(rsum2_ready, 1)
                    elif kind == "add2":
                        u = u2[:, n % 2, :]
                        dve.wait_ge(e2_done, T(8, 4 * h + n + 1, -1))
                        link(dve.tensor_tensor(u, u, e2[:, n % 2, :], ALU.add))
                        link(dve.tensor_tensor(u, u, act2[:, h * TH + n, :], ALU.add))
                        dve.wait_ge(y_loaded[h], T(16, 0))
                        link(dve.scalar_tensor_tensor(y[:, h, n, :], u, 0.0, y[:, h, n, :], ALU.max, ALU.add))
                        link(dve.bn_stats(stats[:, n % 2, :], y[:, h, n, :]), alone=True)
                        dve.bn_aggr(moments[:, n, :], stats[:, n % 2, :]).then_inc(moments_ready, 1)
                    elif kind == "var2":
                        dve.wait_ge(moments_ready, T(8, 4 * h + 4, -1))
                        dve.tensor_scalar(var_eps[:], moments[:, :, 1], LN_EPS, None, ALU.add).then_inc(var_ready, 1)
                    elif kind == "shift2":
                        dve.wait_ge(rstd_ready, T(2, h + 1, -1))
                        dve.scalar_tensor_tensor(shift[:], moments[:, :, 0], -1.0, rstd[:], ALU.mult, ALU.mult)\
                           .then_inc(shift_ready, 1)
                assert links == links_of(steps), (links, links_of(steps))

            dve.wait_ge(keys_set, 12)
            run(FRONT, Turn(dve, -1), 0)
            base = links_of(FRONT)
            run(FIRST, Turn(dve, 0), base)
            base += links_of(FIRST)
            with dve.Fori(1, NB - 1) as b:
                T = Turn(dve, b)
                run(STEADY, T, T(links_of(STEADY), base, -1))
            base += (NB - 2) * links_of(STEADY)
            run(FINISH, Turn(dve, NB - 1), base)
            run(LAST, Turn(dve, NB), base + links_of(FINISH))


NAMES = ["x", "adj", "L0_gnn_mlp1_w", "L0_gnn_mlp1_b", "L0_gnn_mlp2_w", "L0_gnn_mlp2_b", "L0_gnn_W_fc",
         "L0_gnn_a_fc", "L0_gnn_W_hand", "L0_gnn_a_hand"]


def kernel(**inputs):
    import numpy as np
    import concourse.bacc as bacc
    from concourse.bass_utils import run_bass_kernel_spmd

    nc = bacc.Bacc("TRN2", target_bir_lowering=False, num_devices=1)
    arrays, args = {}, []
    for name in NAMES:
        a = np.ascontiguousarray(inputs[name])
        arrays[name + "_dram"] = a
        args.append(nc.dram_tensor(name + "_dram", a.shape, mybir.dt.from_np(a.dtype), kind="ExternalInput").ap())
    out = nc.dram_tensor("out_dram", inputs["x"].shape, F32, kind="ExternalOutput").ap()
    build(nc, *args, out)
    result = run_bass_kernel_spmd(nc, [arrays], core_ids=[0])
    return result.results[0]["out_dram"]
```

```python
from contextlib import ExitStack

import concourse.bass as bass
from concourse import mybir

F32 = mybir.dt.float32
F32R = mybir.dt.float32r
I32 = mybir.dt.int32
U8 = mybir.dt.uint8
ALU = mybir.AluOpType
ACT = mybir.ActivationFunctionType
AX = mybir.AxisListType
ALL_MAX = bass.bass_isa.ReduceOp.max

P = 128
BANK = 512
SLOPE = 0.2
NEG_INF = -9000000000000000.0
RATIO_CAP = 75.0
LN_EPS = 1e-5

ATT1_BANKS = ((0, 1, 2, 3), (4, 5, 6, 7))
SUM_BANK = (4, 0)
SUM_AT = 5
ATT2_BANKS = (4, 5, 6, 7)
MLP2_BANKS = (2, 3)
XT_BANKS = (0, 1)
MLP1_BANKS = (2, 3, 0, 1)
ROLL_BANKS = (4, 5, 3, 0)
KEY2_BANK, KEY1_BANK = 1, 2
SLOTS = 6
GAP_ROW, KEY_ROW, ALPHA_ROW, BETA_ROW = 1, 6, 4, 6


ITEMS = 4
TILES = 8


def chain(kinds, lags, h, n, t):
    return [(t + lag, kind, h, n) for kind, lag in zip(kinds, lags)]


def unit1(at, h, n, t):
    return chain(("full1", "sum1", "hi1", "lo1"), at["unit1_lags"], h, n, t)


def unit2(at, h, n):
    return chain(("slope2", "top2", "exp2", "hi2", "lo2"), at["unit2_lags"], h, n,
                 at["unit2"][h] + at["unit2_pitch"][h] * n)


def after1(at, h, n):
    return chain(("norm1", "low1", "elu1", "elu_elu1", "add1", "hi_post", "lo_post"), at["after1_lags"], h, n,
                 at["after1"][h] + at["after1_pitch"][h] * n)


def before2(at, h, n):
    t = at["before2"][h] + at["before2_pitch"][h] * n
    return chain(("rsum2", "part2"), (0.0, 0.4), h, n, t) if n == 0 else [(t + 0.4, "part2", h, n)]


def after2(at, h, n):
    return chain(("low2", "elu2", "elu_elu2", "add2"), at["after2_lags"], h, n,
                 at["after2"][h] + at["after2_pitch"][h] * n)


def layer_norm(h, t):
    return [(t, "var2", h, 0), (t + 2.0, "shift2", h, 0), (t + 2.5, "scale2", h, 0)]


def next_graph(at):
    steps = []
    for h in range(2):
        for k in range(2):
            steps += chain(("xt", "lo_xt"), at["xt_lags"], h, k, at["xt"][h] + 0.8 * k)
        for f in range(ITEMS):
            t = at["relu1"][h] + at["relu1_pitch"] * f
            steps += chain(("relu1", "hi_act1", "lo_act1"), at["act1_lags"], h, f, t)
        steps += [(at["key_rows"][h], "key_rows", h, 0)]
    steps += [(at["keys1"], "keys1", 0, 0), (at["keys1"] + 2, "gap1", 0, 0), (at["keys1"] + 2.5, "exp1", 0, 0),
              (at["ratio1"], "ratio1", 0, 0)]
    for n in range(TILES):
        t = at["h"] + at["h_pitch"] * n + (at["h_pause"] if n > 1 else 0)
        steps += chain(("hi_h", "lo_h"), at["h_lags"], 0, n, t)
    for n in range(SLOTS):
        steps += unit1(at, 0, n, at["unit10"] + at["unit10_pitch"] * n)
    return steps


def timetable(second, nxt, at):
    steps = []
    for h in range(2):
        steps += [(at["rcol1"][h], "rcol1", h, 0), (at["rsum1"][h], "rsum1", h, 0)]
        for n in range(ITEMS):
            steps += after1(at, h, n)
        steps += [(at["relu2"][h] + 0.6 * n, "relu2", h, n) for n in range(2)]
    for n in range(SLOTS, TILES):
        steps += unit1(at, 0, n, at["unit10_rest"] + at["unit10_pitch"] * (n - SLOTS))
    for n in range(TILES):
        steps += unit1(at, 1, n, at["unit11"] + at["unit11_pitch"] * n)
        steps += [(at["seen2"] + at["seen2_pitch"] * n, "seen2", 0, n)]
    for n in range(ITEMS):
        steps += chain(("hi_h2", "lo_h2"), at["h2_lags"], 0, n, at["h2"] + 1.8 * n)
        steps += [(at["residual"] + 0.9 * n, "residual", 0, n)]
    steps += [(at["keys2"], "keys2", 0, 0), (at["keys2"] + 3.0, "lift2", 0, 0), (at["rows2"], "rows2", 0, 0),
              (at["spread2"], "spread2", 0, 0)]
    if second:
        for h in range(2):
            for n in range(TILES):
                steps += unit2(at, h, n)
            for n in range(ITEMS):
                steps += before2(at, h, n)
                steps += after2(at, h, n)
            steps += layer_norm(h, at["layer_norm"][h])
    if nxt:
        steps += next_graph(at)
    return sorted(steps)


FRONT_AT = {"xt": (1.8, 11.4), "relu1": (7.2, 17.4), "relu1_pitch": 0.9, "key_rows": (24.8, 25.4),
            "keys1": 26.6, "ratio1": 31.7, "h": 33.8, "h_pitch": 4.5, "h_pause": 2.5, "unit10": 61.9,
            "unit10_pitch": 5.8, "unit1_lags": (0.0, 0, 1.0, 1.0), "xt_lags": (0.0, 0.7),
            "act1_lags": (0.0, 0.7, 1.4), "h_lags": (0.0, 0.7)}
STEADY_AT = {"unit10_rest": 18.6, "unit2": (61.4, 116.6), "unit2_pitch": (2.5, 2.4), "rcol1": (69.6, 114.3),
             "rsum1": (73.4, 120.1), "unit11": 89.7, "unit11_pitch": 2.8, "before2": (101.4, 151.9),
             "before2_pitch": (0.6, 2.5), "after2": (102.0, 158.9), "after2_pitch": (0.6, 2.4),
             "layer_norm": (110.4, 171.1), "after1": (106.5, 122.0), "after1_pitch": (3.5, 3.7),
             "relu2": (127.6, 160.6), "xt": (125.8, 159.2), "relu1": (136.2, 165.2), "relu1_pitch": 1.4,
             "h2": 176.0, "key_rows": (171.0, 192.9), "keys2": 181.5, "residual": 199.4, "keys1": 198.0,
             "ratio1": 203.2, "h": 200.6, "h_pitch": 2.3, "h_pause": 0, "seen2": 202.9, "seen2_pitch": 0.9,
             "unit10": 208.5, "unit10_pitch": 4.8, "rows2": 210.2, "spread2": 233.3,
             "unit1_lags": (0.0, 3.5, 3.1, 5.7), "unit2_lags": (0.0, 2.3, 4.3, 4.6, 5.6),
             "after1_lags": (0.0, 1.6, 1.7, 2.4, 3.8, 5.7, 6.0), "after2_lags": (0.0, 0.2, 0.2, 2.6),
             "xt_lags": (0.0, 0.7), "act1_lags": (0.0, 0.7, 1.4), "h_lags": (0.0, 0.7), "h2_lags": (0.0, 0.7)}
LAST_AT = {"unit2": (0.8, 36.0), "unit2_pitch": (2.3, 1.8), "before2": (26.9, 54.8),
           "before2_pitch": (3.0, 2.9), "after2": (28.0, 55.2), "after2_pitch": (2.9, 3.0),
           "layer_norm": (41.0, 76.1), "unit2_lags": (0.0, 2.5, 3.3, 3.5, 5.0),
           "after2_lags": (0.0, 1.5, 1.9, 3.0)}


def last_table(at):
    steps = []
    for h in range(2):
        for n in range(TILES):
            steps += unit2(at, h, n)
        for n in range(ITEMS):
            steps += before2(at, h, n)
            steps += after2(at, h, n)
        steps += layer_norm(h, at["layer_norm"][h])
    return sorted(steps)


LINKS = {"top2": 1, "add1": 2, "add2": 4, "keys1": 1, "keys2": 3, "rows2": 5}


def links_of(steps):
    return sum(LINKS.get(kind, 0) for _, kind, _, _ in steps)


def build(nc, x, adj, w1, b1, w2, b2, wf, af, wh, ah, out):
    NB, N, FI = x.shape
    H = w1.shape[1]
    O = w2.shape[1]
    KI, KH, KO, NT = FI // P, H // P, O // P, N // P
    NH = N // BANK
    TH = NT // NH
    ONES = 2
    assert FI == O and NH == 2 and KH == 4 and KO == 2 and KI == 2 and NT == 8 and NB >= 4

    with ExitStack() as ctx:
        def sb(name, shape, dt):
            return ctx.enter_context(nc.sbuf_tensor(name, shape, dt))

        def sem(name):
            return ctx.enter_context(nc.semaphore(name))

        w1_hi = sb("w1_hi", [P, KI, H], F32R)
        w1_lo = sb("w1_lo", [P, KI, H], F32R)
        wf_hi = sb("wf_hi", [P, KH, H], F32R)
        wf_lo = sb("wf_lo", [P, KH, H], F32R)
        w2_hi = sb("w2_hi", [P, KH, O], F32R)
        w2_lo = sb("w2_lo", [P, KH, O], F32R)
        wh_sb = sb("wh_sb", [P, KO, O], F32)
        b1_sb = sb("b1_sb", [P, KH], F32)
        b2_sb = sb("b2_sb", [P, KO], F32)
        v1_sb = sb("v1_sb", [P, KH, 2], F32)
        v1_split = sb("v1_split", [P, KH, 4], F32R)
        add_pair = sb("add_pair", [4, 2], F32)
        v2_sb = sb("v2_sb", [P, KO, 2], F32)
        adj_sb = sb("adj_sb", [P, NT, N], U8)
        hidden = sb("hidden", [P, NT, N], U8)
        ident = sb("ident", [P, P], F32)
        neg_one = sb("neg_one", [P, 1], F32)
        ones = sb("ones", [P, 2], F32)
        neg_half = sb("neg_half", [P, TH], F32)

        x_in = sb("x_in", [P, TH, FI], F32)
        act1_hi = sb("act1_hi", [P, KH, N], F32R)
        act1_lo = sb("act1_lo", [P, KH, N], F32R)
        h_hi = sb("h_hi", [P, NT, H], F32R)
        h_lo = sb("h_lo", [P, NT, H], F32R)
        act2_t = sb("act2_t", [P, KO, N], F32)
        act2 = sb("act2", [P, NT, O], F32)
        h2_hi = sb("h2_hi", [P, NT, O + ONES], F32R)
        h2_lo = sb("h2_lo", [P, NT, O], F32R)
        y = sb("y", [P, TH, O], F32)

        p_hi = sb("p_hi", [P, SLOTS, BANK], F32R)
        p_lo = sb("p_lo", [P, SLOTS, BANK], F32R)
        p_full = sb("p_full", [P, 3, BANK], F32)
        p_sum = sb("p_sum", [P, BANK], F32)
        ratio = sb("ratio", [P, N], F32)
        rsum1 = ratio
        act1_parts = (ratio[:, 0:BANK], p_sum[:])
        key_rows = ratio[0:4, :]
        alpha = sb("alpha", [P, N], F32)
        beta = sb("beta", [P, N], F32)
        u1 = sb("u1", [P, 2, BANK], F32)
        e1 = sb("e1", [P, 2, BANK], F32)
        junk = beta[:, 0:N // 4].bitcast(U8)

        keys1 = sb("keys1", [P, NT, 2], F32)
        keys2 = sb("keys2", [P, NT, 2], F32)
        top1 = sb("top1", [P, 1], F32)
        top1_all = sb("top1_all", [P, 1], F32)
        neg_top = sb("neg_top", [P, 2], F32)
        gap = sb("gap", [P, NT], F32)
        key_exp = sb("key_exp", [P, 2, NT], F32)
        neg_key = sb("neg_key", [P, NT], F32)
        low2 = sb("low2", [P, 1], F32)
        low2_all = sb("low2_all", [P, 1], F32)
        lift = sb("lift", [P, 1], F32)
        key_pos = sb("key_pos", [P, NT], F32)
        seen = sb("seen", [P, NT], F32)
        rcol = sb("rcol", [P, TH], F32)
        lone = sb("lone", [P, NT], F32)
        best = sb("best", [P, NT], F32)
        top2 = sb("top2", [P, NT], F32)
        alpha_col = sb("alpha_col", [P, NT], F32)
        beta_col = sb("beta_col", [P, NT], F32)
        slope_key = sb("slope_key", [P, NT], F32)
        rsum2 = sb("rsum2", [P, TH], F32)
        stats = sb("stats", [P, 2, 6], F32)
        moments = sb("moments", [P, TH, 2], F32)
        var_eps = sb("var_eps", [P, TH], F32)
        rstd = sb("rstd", [P, TH], F32)
        shift = sb("shift", [P, TH], F32)

        ps = ctx.enter_context(nc.psum_tensor("ps", [P, 8, BANK], F32))

        w_loaded, a_loaded = sem("w_loaded"), sem("a_loaded")
        adj_loaded = [sem("adj_loaded0"), sem("adj_loaded1")]
        x_loaded = [sem("x_loaded0"), sem("x_loaded1")]
        y_loaded = [sem("y_loaded0"), sem("y_loaded1")]
        y_stored = [sem("y_stored0"), sem("y_stored1")]
        w_hi_ready, w_ready = sem("w_hi_ready"), sem("w_ready")
        zeroed, consts, ident_set = sem("zeroed"), sem("consts"), sem("ident_set")
        a_used, keys_set, ones_set = sem("a_used"), sem("keys_set"), sem("ones_set")
        adj_seen, adj_turned, adj_used = sem("adj_seen"), sem("adj_turned"), sem("adj_used")
        xt_done, mlp1_done, keys1_done, h_done = sem("xt_done"), sem("mlp1_done"), sem("keys1_done"), sem("h_done")
        sum1_done, mlp2_done = sem("sum1_done"), sem("mlp2_done")
        res_done, h2_done, keys2_done = sem("res_done"), sem("h2_done"), sem("keys2_done")
        gap_spread, row_done = sem("gap_spread"), sem("row_done")
        p1_used, p2_used = sem("p1_used"), sem("p2_used")
        xt_hi_ready, xt_ready = sem("xt_hi_ready"), sem("xt_ready")
        act1_full, act1_hi_ready, act1_ready = sem("act1_full"), sem("act1_hi_ready"), sem("act1_ready")
        key_rows_done, key_rows_read = sem("key_rows_done"), sem("key_rows_read")
        h_hi_ready, h_ready = sem("h_hi_ready"), sem("h_ready")
        keys1_read, top1_ready, top1_shared = sem("keys1_read"), sem("top1_ready"), sem("top1_shared")
        gap_ready, exp_ready, ratio_ready = sem("gap_ready"), sem("exp_ready"), sem("ratio_ready")
        p1_full, p1_hi, p1_ready = sem("p1_full"), sem("p1_hi"), sem("p1_ready")
        waited_pool, waited_dve = sem("waited_pool"), sem("waited_dve")
        rcol_ready, rsum_spread = sem("rcol_ready"), sem("rsum_spread")
        rsum_ready, p1_summed, seen_set = sem("rsum_ready"), sem("p1_summed"), sem("seen_set")
        normed, e1_low, e1_exp, e1_done, post_done = (
            sem("normed"), sem("e1_low"), sem("e1_exp"), sem("e1_done"), sem("post_done"))
        post_full, post_hi = sem("post_full"), sem("post_hi")
        act2_ready, res_ready, h2_hi_ready, h2_ready = (
            sem("act2_ready"), sem("res_ready"), sem("h2_hi_ready"), sem("h2_ready"))
        keys2_read, low2_ready, low2_shared, pos_ready = (
            sem("keys2_read"), sem("low2_ready"), sem("low2_shared"), sem("pos_ready"))
        cols_ready, rows_ready = sem("cols_ready"), sem("rows_ready")
        p2_slope, p2_masked, p2_full, p2_hi, p2_ready = (
            sem("p2_slope"), sem("p2_masked"), sem("p2_full"), sem("p2_hi"), sem("p2_ready"))
        rsum2_ready, e2_low, e2_exp, att2_read, e2_done, moments_ready, shift_ready = (
            sem("rsum2_ready"), sem("e2_low"), sem("e2_exp"), sem("att2_read"), sem("e2_done"),
            sem("moments_ready"), sem("shift_ready"))
        var_ready, rstd_ready, y_ready, dve_link = (
            sem("var_ready"), sem("rstd_ready"), sem("y_ready"), sem("dve_link"))

        class Turn:

            def __init__(self, eng, b):
                self.eng, self.b, self.times = eng, b, {}

            def __call__(self, per, n, ahead=0):
                if isinstance(self.b, int):
                    return (self.b + ahead) * per + n
                if per not in self.times:
                    self.times[per] = self.eng.snap(self.b * per)
                return self.times[per] + (ahead * per + n)

        FRONT, FIRST, STEADY = sorted(next_graph(FRONT_AT)), timetable(False, True, STEADY_AT), timetable(True, True, STEADY_AT)
        FINISH, LAST = timetable(True, False, STEADY_AT), last_table(LAST_AT)

        def nodes(h):
            return slice(h * BANK, (h + 1) * BANK)

        def block_of(n):
            return slice(n * P, (n + 1) * P)

        def ahead1(h, n):
            return 1 if h == 0 and n < SLOTS else 0

        def slot(attention, h, n):
            return (2 * NT * h + NT * (attention - 1) + n) % SLOTS

        def x_part(part, k, h):
            return h_hi[:, 4 * part + 2 * k + h, :]

        def u2(n):
            return u1[:, n // 2, (n % 2) * O:(n % 2 + 1) * O]

        def e2(n):
            return e1[:, n // 2, (n % 2) * O:(n % 2 + 1) * O]

        x_v = x.rearrange("b (h t p) f -> b h p t f", p=P, t=TH)
        out_v = out.rearrange("b (h t p) f -> b h p t f", p=P, t=TH)
        stage = act2[:].rearrange("p t o -> p (t o)").rearrange("p (s n) -> p s n", s=2).bitcast(I32)
        stage_f = (ratio[:], y[:].rearrange("p t o -> p (t o)"))
        w1_stage = alpha[:].rearrange("p (k f) -> p k f", k=KI)
        w2_stage = beta[:].rearrange("p (k f) -> p k f", k=KH)
        wf_stage = act2_t[:].rearrange("p a n -> p (a n)").rearrange("p (k f) -> p k f", k=KH)
        a_rows = p_full[:, 0:2, :]
        a2_rows = u1[:, 0:1, :]
        a_junk = e1[:, 0, :]

        block = ctx.enter_context(nc.Block())

        @block.sync
        def _(sp):
            def load_adj(t):
                if t >= 2:
                    sp.wait_ge(adj_seen, 2 * (t - 1))
                sp.dma_start(stage[:, t % 2, :], adj[t * P:(t + 1) * P, :]).then_inc(adj_loaded[t % 2], 16)

            load_adj(0)
            load_adj(1)
            for dst, src in ((w1_stage, w1), (wf_stage, wf), (w2_stage, w2),
                             (wh_sb[:], wh)):
                sp.dma_start(dst, src.rearrange("(k p) f -> p k f", p=P)).then_inc(w_loaded, 16)
            with nc.allow_non_contiguous_dma(reason="biases, a few hundred elements, once"):
                sp.dma_start(b1_sb[:], b1.rearrange("(k p) -> p k", p=P)).then_inc(w_loaded, 16)
                sp.dma_start(b2_sb[:], b2.rearrange("(k p) -> p k", p=P)).then_inc(w_loaded, 16)
            a_row = af.rearrange("(s f) c -> (c s) f", s=2)
            a2_row = ah.rearrange("(s f) c -> c (s f)", s=2)
            for s in range(2):
                sp.dma_start(a_rows[:, s, :], a_row[s:s + 1, :].to_broadcast([P, H])).then_inc(a_loaded, 16)
            sp.dma_start(a2_rows[:, 0, :], a2_row[0:1, :].to_broadcast([P, 2 * O])).then_inc(a_loaded, 16)
            def load_x(T, b, h, ahead):
                n = T(4, 2 * h, ahead)
                if not isinstance(n, int) or n > 0:
                    sp.wait_ge(xt_done, n)
                sp.dma_start(x_in[:], x_v[b + ahead, h]).then_inc(x_loaded[h], 16)

            def load_y(T, b, h, first=False):
                if h == 1:
                    sp.wait_ge(y_stored[0], T(16, 0))
                elif not first:
                    sp.wait_ge(y_stored[1], T(16, 0, -1))
                sp.dma_start(y[:], x_v[b - 1, h]).then_inc(y_loaded[h], 16)

            def store_y(T, b, h):
                sp.wait_ge(y_ready, T(2, h + 1, -1))
                sp.dma_start(out_v[b - 1, h], y[:]).then_inc(y_stored[h], 16)

            def iteration(b, first=False, nxt=1):
                T = Turn(sp, b)
                load_y(T, b, 0, first)
                store_y(T, b, 0)
                load_y(T, b, 1)
                if nxt:
                    load_x(T, b, 1, 1)
                if nxt > 1:
                    load_x(T, b, 0, 2)
                store_y(T, b, 1)

            load_x(Turn(sp, 0), 0, 0, 0)
            for t in range(2, NT):
                load_adj(t)
            load_x(Turn(sp, 0), 0, 1, 0)
            for h in range(NH):
                load_x(Turn(sp, 0), 0, h, 1)
            load_x(Turn(sp, 0), 0, 0, 2)
            iteration(1, first=True, nxt=2)
            with sp.Fori(2, NB - 2) as b:
                iteration(b, nxt=2)
            iteration(NB - 2, nxt=1)
            iteration(NB - 1, nxt=0)
            iteration(NB, nxt=0)
            for h in range(NH):
                sp.wait_ge(y_stored[h], 16 * NB)

        @block.gpsimd
        def _(pool):
            pool.memset(ident[:], 0.0).then_inc(zeroed, 1)
            pool.wait_ge(zeroed, 1)
            pool.affine_select(out=ident[:], in_=ident[:], compare_op=ALU.not_equal, fill=1.0, base=0,
                               pattern=[[-1, P]], channel_multiplier=1).then_inc(ident_set, 1)
            pool.memset(neg_half[:], -0.5).then_inc(zeroed, 1)
            pool.wait_ge(zeroed, 2)

            def top(T, ahead):
                pool.wait_ge(top1_ready, T(1, 1, ahead))
                pool.sem_inc(waited_pool)
                pool.partition_all_reduce(top1_all[:], top1[:], P, ALL_MAX).then_inc(top1_shared, 1)

            def low(T):
                pool.wait_ge(low2_ready, T(1, 1))
                pool.sem_inc(waited_pool)
                pool.partition_all_reduce(low2_all[:], low2[:], P, ALL_MAX).then_inc(low2_shared, 1)

            def deviation(T, h):
                pool.wait_ge(var_ready, T(2, h + 1, -1))
                pool.tensor_tensor(rstd[:], var_eps[:], neg_half[:], ALU.pow).then_inc(rstd_ready, 1)

            def iteration(b, second=True, nxt=True):
                T = Turn(pool, b)
                if second:
                    deviation(T, 0)
                    deviation(T, 1)
                low(T)
                if nxt:
                    top(T, 1)

            top(Turn(pool, 0), 0)
            iteration(0, second=False)
            with pool.Fori(1, NB - 1) as b:
                iteration(b)
            iteration(NB - 1, nxt=False)
            T = Turn(pool, NB)
            deviation(T, 0)
            deviation(T, 1)

        @block.tensor
        def _(pe):
            def turn_x(T, ahead, h):
                pe.wait_ge(x_loaded[h], T(16, 16, ahead))
                for k in range(KI):
                    for t in range(TH):
                        last = pe.transpose(ps[:, XT_BANKS[k], block_of(t)], x_in[:, t, block_of(k)], ident[:])
                    last.then_inc(xt_done, 1)

            def mlp1(T, ahead, h):
                pe.wait_ge(xt_ready, T(4, 2 * h + 2, ahead))
                for f in range(KH):
                    acc = ps[:, MLP1_BANKS[f], :]
                    for k in range(KI):
                        pe.matmul(acc, w1_hi[:, k, block_of(f)], x_part(0, k, h), start=(k == 0), stop=False)
                        pe.matmul(acc, w1_hi[:, k, block_of(f)], x_part(1, k, h), start=False, stop=False)
                        last = pe.matmul(acc, w1_lo[:, k, block_of(f)], x_part(0, k, h), start=False,
                                         stop=(k == KI - 1))
                    last.then_inc(mlp1_done, 1)

            def find_key_rows(T, ahead, h):
                if h == 1:
                    pe.wait_ge(key_rows_read, T(2, 1, ahead))
                for k in range(KH):
                    pe.matmul(ps[0:4, KEY1_BANK, :], v1_split[:, k, :], act1_hi[:, k, nodes(h)],
                              start=(k == 0), stop=False)
                    last = pe.matmul(ps[0:4, KEY1_BANK, :], v1_split[:, k, :], act1_lo[:, k, nodes(h)],
                                     start=False, stop=(k == KH - 1))
                last.then_inc(key_rows_done, 1)

            def turn_key_rows(T, ahead):
                pe.wait_ge(key_rows_read, T(2, 2, ahead))
                for t in range(NT):
                    last = pe.matmul(ps[:, KEY1_BANK, 2 * t:2 * t + 2], key_rows[:, block_of(t)],
                                     add_pair[:], start=True, stop=True)
                last.then_inc(keys1_done, 1)

            def find_keys2():
                for t in range(NT):
                    for k in range(KO):
                        last = pe.matmul(ps[:, KEY2_BANK, 2 * t:2 * t + 2], act2_t[:, k, block_of(t)],
                                         v2_sb[:, k, :], start=(k == 0), stop=(k == KO - 1))
                last.then_inc(keys2_done, 1)

            def spread(col, bank, done):
                for t in range(NT):
                    last = pe.matmul(ps[:, bank + t // TH, block_of(t % TH)], col[:, t:t + 1].to_broadcast([P, P]),
                                     ident[:], start=True, stop=True)
                last.then_inc(done, 1)

            def h_tile(T, ahead, t):
                if t >= len(ROLL_BANKS):
                    pe.wait_ge(h_ready, T(8, t - 3, ahead))
                acc = ps[:, ROLL_BANKS[t % 4], :]
                for k in range(KH):
                    pe.matmul(acc, act1_hi[:, k, block_of(t)], wf_hi[:, k, :], start=(k == 0), stop=False)
                    pe.matmul(acc, act1_hi[:, k, block_of(t)], wf_lo[:, k, :], start=False, stop=False)
                    last = pe.matmul(acc, act1_lo[:, k, block_of(t)], wf_hi[:, k, :], start=False,
                                     stop=(k == KH - 1))
                last.then_inc(h_done, 1)

            def attend1(T, h, second):
                for j in range(NT):
                    if j == SUM_AT:
                        pe.wait_ge(p1_summed, T(16, 8 * h + 8))
                        if second and h == 0:
                            pe.wait_ge(rows_ready, T(4, 4, -1))
                        if h == 1:
                            pe.wait_ge(normed, T(8, 1))
                        for c in range(TH):
                            last = pe.matmul(ps[:, SUM_BANK[h], c:c + 1], p_sum[:, block_of(c)], ones[:, 0:1],
                                             start=True, stop=True)
                        last.then_inc(sum1_done, 1)
                    if j == SUM_AT + 1:
                        pe.wait_ge(rcol_ready, T(2, h + 1))
                        for c in range(TH):
                            last = pe.matmul(ps[:, SUM_BANK[h], block_of(c)], rcol[:, c:c + 1].to_broadcast([P, P]),
                                             ident[:], start=True, stop=True)
                        last.then_inc(rsum_spread, 1)
                    pe.wait_ge(p1_ready, T(16, 8 * h + j + 1))
                    at = slot(1, h, j)
                    for f in range(KH):
                        acc = ps[:, ATT1_BANKS[h][f], :]
                        if second and h == 1 and j == 0:
                            pe.wait_ge(att2_read, T(8, f + 1, -1))
                        pe.matmul(acc, h_hi[:, j, block_of(f)], p_hi[:, at, :], start=(j == 0), stop=False)
                        pe.matmul(acc, h_hi[:, j, block_of(f)], p_lo[:, at, :], start=False, stop=False)
                        last = pe.matmul(acc, h_lo[:, j, block_of(f)], p_hi[:, at, :], start=False, stop=(j == NT - 1))
                    last.then_inc(p1_used, 1)

            def attend2(T, h):
                for j in range(NT):
                    pe.wait_ge(p2_ready, T(16, 8 * h + j + 1, -1))
                    at = slot(2, h, j)
                    for q in range(TH):
                        acc = ps[:, ATT2_BANKS[q], 0:O + ONES]
                        pe.matmul(acc, p_hi[:, at, block_of(q)], h2_hi[:, j, :], start=(j == 0), stop=False)
                        pe.matmul(acc, p_lo[:, at, block_of(q)], h2_hi[:, j, :], start=False, stop=False)
                        last = pe.matmul(ps[:, ATT2_BANKS[q], 0:O], p_hi[:, at, block_of(q)], h2_lo[:, j, :],
                                         start=False, stop=(j == NT - 1))
                    last.then_inc(p2_used, 1)

            def mlp2(T, h):
                pe.wait_ge(post_done, T(8, 4 * h + 4))
                for o in range(KO):
                    acc = ps[:, MLP2_BANKS[o], :]
                    for k in range(KH):
                        pe.matmul(acc, w2_hi[:, k, block_of(o)], act1_hi[:, k, nodes(h)], start=(k == 0), stop=False)
                        pe.matmul(acc, w2_hi[:, k, block_of(o)], act1_lo[:, k, nodes(h)], start=False, stop=False)
                        last = pe.matmul(acc, w2_lo[:, k, block_of(o)], act1_hi[:, k, nodes(h)], start=False,
                                         stop=(k == KH - 1))
                    last.then_inc(mlp2_done, 1)

            def iteration(b, second=True, nxt=True):
                T = Turn(pe, b)
                pe.wait_ge(h_ready, T(8, 8))
                pe.wait_ge(ratio_ready, T(2, 2))
                attend1(T, 0, second)
                pe.wait_ge(rsum_ready, T(2, 1))
                if second:
                    attend2(T, 0)
                attend1(T, 1, second)
                pe.wait_ge(rsum_ready, T(2, 2))
                pe.wait_ge(normed, T(8, 2))
                if nxt:
                    turn_x(T, 1, 0)
                mlp2(T, 0)
                if nxt:
                    pe.wait_ge(act2_ready, T(4, 2))
                    mlp1(T, 1, 0)
                if second:
                    pe.wait_ge(normed, T(8, 8))
                    attend2(T, 1)
                if nxt:
                    pe.wait_ge(act1_full, T(8, 4, 1))
                    turn_x(T, 1, 1)
                else:
                    pe.wait_ge(act2_ready, T(4, 2))
                mlp2(T, 1)
                pe.wait_ge(act2_ready, T(4, 4))
                if nxt:
                    mlp1(T, 1, 1)
                if second:
                    pe.wait_ge(att2_read, T(8, 8, -1))
                else:
                    pe.wait_ge(normed, T(8, 8))
                for n in range(4):
                    if nxt and n == 2:
                        pe.wait_ge(act1_full, T(8, 8, 1))
                    for t in (2 * n, 2 * n + 1):
                        for k in range(KO):
                            last = pe.matmul(ps[:, ROLL_BANKS[n], (t % 2) * O:(t % 2 + 1) * O],
                                             act2_t[:, k, block_of(t)], wh_sb[:, k, :],
                                             start=(k == 0), stop=(k == KO - 1))
                    last.then_inc(h2_done, 1)
                if nxt:
                    pe.wait_ge(act1_ready, T(8, 8, 1))
                    find_key_rows(T, 1, 0)
                find_keys2()
                if nxt:
                    find_key_rows(T, 1, 1)
                for n in range(4):
                    pe.wait_ge(h2_ready, T(4, n + 1))
                    for t in (2 * n, 2 * n + 1):
                        for o in range(KO):
                            at = (t % 2) * O + o * P
                            last = pe.transpose(ps[:, ROLL_BANKS[n], at:at + P], act2_t[:, o, block_of(t)], ident[:])
                    last.then_inc(res_done, 1)
                if nxt:
                    turn_key_rows(T, 1)
                    for t in range(2):
                        pe.wait_ge(res_ready, T(4, t + 1))
                        h_tile(T, 1, t)
                    pe.wait_ge(gap_ready, T(1, 1, 1))
                    pe.wait_ge(keys2_read, T(1, 1))
                    spread(gap, GAP_ROW, gap_spread)
                pe.wait_ge(pos_ready, T(1, 1))
                spread(key_pos, KEY_ROW, row_done)
                if nxt:
                    for t in range(2, NT):
                        if t < 4:
                            pe.wait_ge(res_ready, T(4, t + 1))
                        h_tile(T, 1, t)
                pe.wait_ge(cols_ready, T(1, 1))
                if nxt:
                    pe.wait_ge(h_ready, T(8, 6, 1))
                else:
                    pe.wait_ge(res_ready, T(4, 2))
                spread(alpha_col, ALPHA_ROW, row_done)
                spread(beta_col, BETA_ROW, row_done)

            pe.wait_ge(ident_set, 1)
            pe.wait_ge(consts, 3)
            for t in range(NT):
                pe.wait_ge(adj_seen, 2 * (t + 1))
                for h in range(NH):
                    if t >= 2:
                        pe.wait_ge(adj_used, 2 * (t - 1) + h - 1)
                    for j in range(TH):
                        last = pe.transpose(ps[:, 4 * (t % 2) + h, block_of(j)],
                                            stage_f[t % 2][:, block_of(h * TH + j)], ident[:])
                    last.then_inc(adj_turned, 1)
            pe.wait_ge(w_ready, 3)
            pe.wait_ge(adj_used, 16)
            T = Turn(pe, 0)
            turn_x(T, 0, 0)
            mlp1(T, 0, 0)
            pe.wait_ge(act1_full, 4)
            turn_x(T, 0, 1)
            mlp1(T, 0, 1)
            pe.wait_ge(act1_ready, 8)
            pe.wait_ge(w_ready, 5)
            find_key_rows(T, 0, 0)
            find_key_rows(T, 0, 1)
            turn_key_rows(T, 0)
            h_tile(T, 0, 0)
            h_tile(T, 0, 1)
            pe.wait_ge(gap_ready, 1)
            spread(gap, GAP_ROW, gap_spread)
            for t in range(2, NT):
                h_tile(T, 0, t)

            iteration(0, second=False)
            with pe.Fori(1, NB - 1) as b:
                iteration(b)
            iteration(NB - 1, nxt=False)
            T = Turn(pe, NB)
            pe.wait_ge(rows_ready, 4 * NB)
            pe.wait_ge(h2_ready, 4 * NB)
            attend2(T, 0)
            pe.wait_ge(att2_read, T(8, 4, -1))
            attend2(T, 1)

        @block.scalar
        def _(act):
            act.wait_ge(consts, 3)
            for t in range(NT):
                act.activation(h2_hi[:, t, O:O + ONES], ones[:, 0:ONES], ACT.Copy).then_inc(ones_set, 1)
            act.wait_ge(w_loaded, 96)
            for w_hi, staged in ((w1_hi, w1_stage), (w2_hi, w2_stage), (wf_hi, wf_stage)):
                act.activation(w_hi[:], staged, ACT.Copy).then_inc(w_hi_ready, 1)
            act.wait_ge(keys_set, 12)
            act.activation(v1_split[:, :, 0:2], v1_sb[:], ACT.Copy).then_inc(w_hi_ready, 1)

            def run(steps, T):
                for _, kind, h, n in steps:
                    if kind == "xt":
                        act.wait_ge(xt_done, T(4, 2 * h + n + 1, 1))
                        act.activation(x_part(0, n, h), ps[:, XT_BANKS[n], :], ACT.Copy).then_inc(xt_hi_ready, 1)
                    elif kind == "relu1":
                        act.wait_ge(mlp1_done, T(8, 4 * h + n + 1, 1))
                        if n >= 2 or h == 1:
                            act.wait_ge(act1_ready, T(8, 4 * h + n - 1, 1))
                        act.activation(act1_parts[n % 2], ps[:, MLP1_BANKS[n], :], ACT.Relu,
                                       bias=b1_sb[:, n:n + 1]).then_inc(act1_full, 1)
                    elif kind == "hi_act1":
                        act.wait_ge(act1_full, T(8, 4 * h + n + 1, 1))
                        act.activation(act1_hi[:, n, nodes(h)], act1_parts[n % 2], ACT.Copy)\
                           .then_inc(act1_hi_ready, 1)
                    elif kind == "key_rows":
                        act.wait_ge(key_rows_done, T(2, h + 1, 1))
                        act.activation(key_rows[:, nodes(h)], ps[0:4, KEY1_BANK, :], ACT.Copy)\
                           .then_inc(key_rows_read, 1)
                    elif kind == "hi_h":
                        act.wait_ge(h_done, T(8, n + 1, 1))
                        act.activation(h_hi[:, n, :], ps[:, ROLL_BANKS[n % 4], :], ACT.Copy).then_inc(h_hi_ready, 1)
                    elif kind == "exp1":
                        act.wait_ge(gap_ready, T(1, 1, 1))
                        act.activation(key_exp[:, 0, :], keys1[:, :, 1], ACT.Exp, bias=neg_top[:, 0:1])
                        act.activation(key_exp[:, 1, :], keys1[:, :, 1], ACT.Exp, bias=neg_top[:, 1:2],
                                       scale=SLOPE).then_inc(exp_ready, 1)
                    elif kind == "ratio1":
                        act.wait_ge(gap_spread, T(1, 1, 1))
                        for half in range(NH):
                            act.activation(ratio[:, nodes(half)], ps[:, GAP_ROW + half, :], ACT.Exp,
                                           scale=1.0 - SLOPE).then_inc(ratio_ready, 1)
                    elif kind == "hi1":
                        act.wait_ge(p1_full, T(16, 8 * h + n + 1, ahead1(h, n)))
                        if n >= SLOTS:
                            act.wait_ge(p1_used, T(16, 8 * h + n + 1 - SLOTS))
                        elif h == 1 and first_turn:
                            act.wait_ge(p1_used, T(16, NT))
                        elif h == 1:
                            act.wait_ge(p2_used, T(16, NT + n + 1 - SLOTS, -1))
                        act.activation(p_hi[:, slot(1, h, n), :], p_full[:, n % 3, :], ACT.Copy).then_inc(p1_hi, 1)
                    elif kind == "low1":
                        act.wait_ge(normed, T(8, 4 * h + n + 1))
                        act.activation(e1[:, n % 2, :], u1[:, n % 2, :], ACT.Relu, scale=-1.0).then_inc(e1_low, 1)
                    elif kind == "elu1":
                        act.wait_ge(e1_low, T(8, 4 * h + n + 1))
                        act.activation(e1[:, n % 2, :], e1[:, n % 2, :], ACT.Exp, scale=-1.0).then_inc(e1_exp, 1)
                    elif kind == "elu_elu1":
                        act.wait_ge(e1_exp, T(8, 4 * h + n + 1))
                        act.activation(e1[:, n % 2, :], e1[:, n % 2, :], ACT.Exp, bias=neg_one[:]).then_inc(e1_done, 1)
                    elif kind == "rsum1":
                        act.wait_ge(rsum_spread, T(2, h + 1))
                        act.activation(rsum1[:, nodes(h)], ps[:, SUM_BANK[h], :], ACT.Copy).then_inc(rsum_ready, 1)
                    elif kind == "hi_post":
                        act.wait_ge(post_full, T(8, 4 * h + n + 1))
                        act.activation(act1_hi[:, n, nodes(h)], u1[:, n % 2, :], ACT.Copy).then_inc(post_hi, 1)
                    elif kind == "relu2":
                        act.wait_ge(mlp2_done, T(4, 2 * h + n + 1))
                        act.activation(act2_t[:, n, nodes(h)], ps[:, MLP2_BANKS[n], :], ACT.Relu,
                                       bias=b2_sb[:, n:n + 1]).then_inc(act2_ready, 1)
                    elif kind == "residual":
                        act.wait_ge(res_done, T(4, n + 1))
                        if n == 0 and not first_turn:
                            act.wait_ge(moments_ready, T(8, 8, -1))
                        act.activation(act2[:, 2 * n:2 * n + 2, :],
                                       ps[:, ROLL_BANKS[n], :].rearrange("p (t o) -> p t o", t=2),
                                       ACT.Identity, bias=neg_one[:]).then_inc(res_ready, 1)
                    elif kind == "hi_h2":
                        act.wait_ge(h2_done, T(4, n + 1))
                        act.activation(h2_hi[:, 2 * n:2 * n + 2, 0:O],
                                       ps[:, ROLL_BANKS[n], :].rearrange("p (t o) -> p t o", t=2),
                                       ACT.Copy).then_inc(h2_hi_ready, 1)
                    elif kind == "spread2":
                        act.wait_ge(row_done, T(3, 3))
                        for half in range(NH):
                            act.activation(alpha[:, nodes(half)], ps[:, ALPHA_ROW + half, :], ACT.Copy)\
                               .then_inc(rows_ready, 1)
                            act.activation(beta[:, nodes(half)], ps[:, BETA_ROW + half, :], ACT.Copy)\
                               .then_inc(rows_ready, 1)
                    elif kind == "slope2":
                        if n == 0 and h == 0:
                            act.wait_ge(rows_ready, T(4, 0))
                        if n == 0 and h == 1 and last_turn:
                            act.wait_ge(p2_ready, T(16, 8, -1))
                        elif n == 0:
                            act.wait_ge(p1_ready, T(16, 0 if last_turn else 8 * h + 8))
                        if n >= 3:
                            act.wait_ge(p2_ready, T(16, 8 * h + n - 2, -1))
                        act.activation(p_full[:, n % 3, :], beta[:, nodes(h)], ACT.Identity,
                                       bias=slope_key[:, n:n + 1]).then_inc(p2_slope, 1)
                    elif kind == "exp2":
                        act.wait_ge(p2_masked, T(16, 8 * h + n + 1, -1))
                        act.activation(p_full[:, n % 3, :], p_full[:, n % 3, :], ACT.Exp).then_inc(p2_full, 1)
                    elif kind == "hi2":
                        act.wait_ge(p2_full, T(16, 8 * h + n + 1, -1))
                        if n >= SLOTS:
                            act.wait_ge(p2_used, T(16, 8 * h + n + 1 - SLOTS, -1))
                        elif not last_turn:
                            act.wait_ge(p1_used, T(16, 8 * h + NT + n + 1 - SLOTS))
                        elif h == 0:
                            act.wait_ge(p1_used, T(16, 0))
                        else:
                            before = max(m for m in range(NT) if slot(2, 0, m) == slot(2, 1, n))
                            act.wait_ge(p2_used, T(16, before + 1, -1))
                        act.activation(p_hi[:, slot(2, h, n), :], p_full[:, n % 3, :], ACT.Copy).then_inc(p2_hi, 1)
                    elif kind == "part2":
                        act.wait_ge(rsum2_ready, T(2, h + 1, -1))
                        if h == 1 and last_turn:
                            act.wait_ge(moments_ready, T(8, n + 1, -1))
                        elif h == 1:
                            act.wait_ge(post_done, T(8, 8))
                        act.activation(u2(n), ps[:, ATT2_BANKS[n], 0:O], ACT.Copy,
                                       scale=rsum2[:, n:n + 1]).then_inc(att2_read, 1)
                    elif kind == "low2":
                        act.wait_ge(att2_read, T(8, 4 * h + n + 1, -1))
                        act.activation(e2(n), u2(n), ACT.Relu, scale=-1.0).then_inc(e2_low, 1)
                    elif kind == "elu2":
                        act.wait_ge(e2_low, T(8, 4 * h + n + 1, -1))
                        act.activation(e2(n), e2(n), ACT.Exp, scale=-1.0).then_inc(e2_exp, 1)
                    elif kind == "elu_elu2":
                        act.wait_ge(e2_exp, T(8, 4 * h + n + 1, -1))
                        act.activation(e2(n), e2(n), ACT.Exp, bias=neg_one[:]).then_inc(e2_done, 1)
                    elif kind == "scale2":
                        act.wait_ge(shift_ready, T(2, h + 1, -1))
                        for t in range(TH):
                            ins = act.activation(y[:, t, :], y[:, t, :], ACT.Identity,
                                                 bias=shift[:, t:t + 1], scale=rstd[:, t:t + 1])
                        ins.then_inc(y_ready, 1)

            last_turn, first_turn = False, True
            run(FRONT, Turn(act, -1))
            run(FIRST, Turn(act, 0))
            first_turn = False
            with act.Fori(1, NB - 1) as b:
                run(STEADY, Turn(act, b))
            run(FINISH, Turn(act, NB - 1))
            last_turn = True
            run(LAST, Turn(act, NB))

        @block.vector
        def _(dve):
            dve.memset(ones[:], 1.0).then_inc(consts, 1)
            dve.memset(neg_one[:], -1.0).then_inc(consts, 1)
            dve.memset(p_sum[:], 0.0).then_inc(consts, 1)
            for t in range(NT):
                dve.wait_ge(adj_loaded[t % 2], 16 * (t // 2 + 1))
                if t >= 2:
                    dve.wait_ge(adj_turned, 2 * (t - 1))
                dve.tensor_scalar(adj_sb[:, t, :], stage[:, t % 2, :], 0.0, None, ALU.is_gt).then_inc(adj_seen, 1)
                dve.tensor_scalar(stage_f[t % 2], stage[:, t % 2, :], 0.0, None, ALU.is_gt).then_inc(adj_seen, 1)
                if t >= 1:
                    turned_tile = t - 1
                    for h in range(NH):
                        dve.wait_ge(adj_turned, 2 * turned_tile + h + 1)
                        dve.tensor_scalar(hidden[:, h * TH:(h + 1) * TH, block_of(turned_tile)],
                                          ps[:, 4 * (turned_tile % 2) + h, :].rearrange("p (j i) -> p j i", j=TH),
                                          0.5, None, ALU.is_lt).then_inc(adj_used, 1)
            for h in range(NH):
                dve.wait_ge(adj_turned, 2 * (NT - 1) + h + 1)
                dve.tensor_scalar(hidden[:, h * TH:(h + 1) * TH, block_of(NT - 1)],
                                  ps[:, 4 * ((NT - 1) % 2) + h, :].rearrange("p (j i) -> p j i", j=TH),
                                  0.5, None, ALU.is_lt).then_inc(adj_used, 1)
            for n, (w_lo, w_hi, staged) in enumerate(((w1_lo, w1_hi, w1_stage), (w2_lo, w2_hi, w2_stage),
                                                      (wf_lo, wf_hi, wf_stage))):
                dve.wait_ge(w_hi_ready, n + 1)
                dve.tensor_tensor(w_lo[:], staged, w_hi[:].bitcast(F32), ALU.subtract).then_inc(w_ready, 1)
            dve.wait_ge(a_loaded, 48)
            dve.wait_ge(w_loaded, 96)
            for k in range(KH):
                for s in range(2):
                    if k + s:
                        dve.wait_ge(keys_set, 2 * k + s)
                    dve.tensor_tensor_reduce(out=a_junk, in0=wf_stage[:, k, :], in1=a_rows[:, s, :], scale=1.0,
                                             scalar=0.0, op0=ALU.mult, op1=ALU.add,
                                             accum_out=v1_sb[:, k, s:s + 1]).then_inc(keys_set, 1)
            for k in range(KO):
                for s in range(2):
                    dve.wait_ge(keys_set, 2 * KH + 2 * k + s)
                    dve.tensor_tensor_reduce(out=a_junk[:, 0:O], in0=wh_sb[:, k, :],
                                             in1=a2_rows[:, 0, s * O:(s + 1) * O], scale=1.0,
                                             scalar=0.0, op0=ALU.mult, op1=ALU.add,
                                             accum_out=v2_sb[:, k, s:s + 1]).then_inc(keys_set, 1)
            dve.wait_ge(keys_set, 12)
            dve.wait_ge(w_hi_ready, 4)
            dve.tensor_tensor(v1_split[:, :, 2:4], v1_sb[:], v1_split[:, :, 0:2].bitcast(F32), ALU.subtract)\
               .then_inc(w_ready, 1)
            dve.wait_ge(ident_set, 1)
            dve.tensor_tensor(add_pair[:], ident[0:4, 0:2], ident[0:4, 2:4], ALU.add).then_inc(w_ready, 1)

            def run(steps, T, link_base, first_turn=False):
                links = 0

                def link(ins, alone=False):
                    nonlocal links
                    ins.then_inc(dve_link, 1)
                    links += 1
                    dve.wait_ge(dve_link, link_base + links)
                    if alone:
                        dve.sem_inc(waited_dve)

                for _, kind, h, n in steps:
                    if kind == "lo_xt":
                        dve.wait_ge(xt_hi_ready, T(4, 2 * h + n + 1, 1))
                        dve.tensor_tensor(x_part(1, n, h), ps[:, XT_BANKS[n], :], x_part(0, n, h).bitcast(F32),
                                          ALU.subtract).then_inc(xt_ready, 1)
                    elif kind == "lo_act1":
                        dve.wait_ge(act1_hi_ready, T(8, 4 * h + n + 1, 1))
                        dve.tensor_tensor(act1_lo[:, n, nodes(h)], act1_parts[n % 2],
                                          act1_hi[:, n, nodes(h)].bitcast(F32), ALU.subtract).then_inc(act1_ready, 1)
                    elif kind == "lo_h":
                        dve.wait_ge(h_hi_ready, T(8, n + 1, 1))
                        dve.tensor_tensor(h_lo[:, n, :], ps[:, ROLL_BANKS[n % 4], :], h_hi[:, n, :].bitcast(F32),
                                          ALU.subtract).then_inc(h_ready, 1)
                    elif kind == "keys1":
                        dve.wait_ge(keys1_done, T(1, 1, 1))
                        link(dve.tensor_copy(keys1[:].rearrange("p t s -> p (t s)"), ps[:, KEY1_BANK, 0:2 * NT]))
                        dve.tensor_reduce(top1[:], keys1[:, :, 1], AX.X, ALU.max).then_inc(top1_ready, 1)
                    elif kind == "gap1":
                        dve.wait_ge(top1_shared, T(1, 1, 1))
                        dve.tensor_scalar(neg_top[:, 0:1], top1_all[:], -1.0, None, ALU.mult)
                        dve.tensor_scalar(neg_top[:, 1:2], top1_all[:], -SLOPE, None, ALU.mult)
                        dve.tensor_scalar(gap[:], keys1[:, :, 0], top1_all[:], RATIO_CAP, ALU.add, ALU.min)\
                           .then_inc(gap_ready, 1)
                    elif kind == "full1":
                        if h == 0 and n == 0:
                            dve.wait_ge(exp_ready, T(1, 1, 1))
                            dve.wait_ge(ratio_ready, T(2, 2, 1))
                        if n >= 3:
                            dve.wait_ge(p1_ready, T(16, 8 * h + n - 2, ahead1(h, n)))
                        elif h == 1 and first_turn:
                            dve.wait_ge(p1_ready, T(16, 8))
                        elif h == 1:
                            dve.wait_ge(p2_ready, T(16, 8, -1))
                        dve.tensor_scalar(p_full[:, n % 3, :], ratio[:, nodes(h)], key_exp[:, 0, n:n + 1],
                                          key_exp[:, 1, n:n + 1], ALU.mult, ALU.max).then_inc(p1_full, 1)
                    elif kind == "sum1":
                        dve.wait_ge(p1_full, T(16, 8 * h + n + 1, ahead1(h, n)))
                        if n == 0:
                            before = T(2, h, ahead1(h, n))
                            if not isinstance(before, int) or before > 0:
                                dve.wait_ge(sum1_done, before)
                            ins = dve.tensor_copy(p_sum[:], p_full[:, n % 3, :])
                        else:
                            dve.wait_ge(p1_summed, T(16, 8 * h + n, ahead1(h, n)))
                            ins = dve.tensor_tensor(p_sum[:], p_sum[:], p_full[:, n % 3, :], ALU.add)
                        ins.then_inc(p1_summed, 1)
                    elif kind == "lo1":
                        dve.wait_ge(p1_hi, T(16, 8 * h + n + 1, ahead1(h, n)))
                        dve.tensor_tensor(p_lo[:, slot(1, h, n), :], p_full[:, n % 3, :],
                                          p_hi[:, slot(1, h, n), :].bitcast(F32), ALU.subtract).then_inc(p1_ready, 1)
                    elif kind == "rcol1":
                        dve.wait_ge(sum1_done, T(2, h + 1))
                        dve.reciprocal(rcol[:], ps[:, SUM_BANK[h], 0:TH]).then_inc(rcol_ready, 1)
                    elif kind == "norm1":
                        if n >= 2 or h == 1:
                            dve.wait_ge(post_done, T(8, 4 * h + n - 1))
                        elif not first_turn:
                            dve.wait_ge(moments_ready, T(8, 4, -1))
                        dve.wait_ge(rsum_ready, T(2, h + 1))
                        dve.wait_ge(p1_used, T(16, 8 * h + 8))
                        dve.tensor_tensor(u1[:, n % 2, :], ps[:, ATT1_BANKS[h][n], :], rsum1[:, nodes(h)], ALU.mult)\
                           .then_inc(normed, 1)
                    elif kind == "add1":
                        dve.wait_ge(e1_done, T(8, 4 * h + n + 1))
                        link(dve.scalar_tensor_tensor(u1[:, n % 2, :], u1[:, n % 2, :], 0.0, e1[:, n % 2, :],
                                                      ALU.max, ALU.add))
                        link(dve.tensor_tensor(u1[:, n % 2, :], u1[:, n % 2, :], act1_hi[:, n, nodes(h)].bitcast(F32),
                                               ALU.add))
                        dve.scalar_tensor_tensor(u1[:, n % 2, :], u1[:, n % 2, :], -1.0,
                                                 act1_lo[:, n, nodes(h)].bitcast(F32),
                                                 ALU.add, ALU.add).then_inc(post_full, 1)
                    elif kind == "lo_post":
                        dve.wait_ge(post_hi, T(8, 4 * h + n + 1))
                        dve.tensor_tensor(act1_lo[:, n, nodes(h)], u1[:, n % 2, :],
                                          act1_hi[:, n, nodes(h)].bitcast(F32), ALU.subtract).then_inc(post_done, 1)
                    elif kind == "lo_h2":
                        dve.wait_ge(h2_hi_ready, T(4, n + 1))
                        dve.tensor_tensor(h2_lo[:, 2 * n:2 * n + 2, :],
                                          ps[:, ROLL_BANKS[n], :].rearrange("p (t o) -> p t o", t=2),
                                          h2_hi[:, 2 * n:2 * n + 2, 0:O].bitcast(F32),
                                          ALU.subtract).then_inc(h2_ready, 1)
                    elif kind == "keys2":
                        dve.wait_ge(keys2_done, T(1, 1))
                        dve.tensor_copy(keys2[:].rearrange("p t s -> p (t s)"), ps[:, KEY2_BANK, 0:2 * NT])\
                           .then_inc(keys2_read, 1)
                        dve.wait_ge(keys2_read, T(1, 1))
                        link(dve.tensor_scalar(neg_key[:], keys2[:, :, 1], -1.0, None, ALU.mult))
                        link(dve.tensor_scalar(slope_key[:], keys2[:, :, 1], SLOPE, None, ALU.mult))
                        dve.tensor_reduce(low2[:], neg_key[:], AX.X, ALU.max).then_inc(low2_ready, 1)
                        link(dve.tensor_scalar(best[:], keys2[:, :, 0], SLOPE, None, ALU.mult))
                    elif kind == "lift2":
                        dve.wait_ge(low2_shared, T(1, 1))
                        dve.tensor_scalar(lift[:], low2_all[:], 1.0, None, ALU.add)
                        dve.tensor_scalar(key_pos[:], keys2[:, :, 1], low2_all[:], 1.0, ALU.add, ALU.add)\
                           .then_inc(pos_ready, 1)
                    elif kind == "seen2":
                        if n == 0:
                            dve.wait_ge(row_done, T(3, 1))
                        else:
                            dve.wait_ge(seen_set, T(8, n))
                        dve.sem_inc(waited_dve)
                        dve.tensor_tensor_reduce(out=junk, in0=adj_sb[:, n, :],
                                                 in1=ps[:, KEY_ROW:KEY_ROW + 2, :].rearrange("p a b -> p (a b)"),
                                                 scale=1.0, scalar=0.0, op0=ALU.mult, op1=ALU.max,
                                                 accum_out=seen[:, n:n + 1]).then_inc(seen_set, 1)
                    elif kind == "rows2":
                        dve.wait_ge(seen_set, T(8, 8))
                        dve.tensor_scalar(lone[:], seen[:], 0.5, NEG_INF, ALU.is_lt, ALU.mult)
                        link(dve.tensor_scalar(best[:], seen[:], lift[:], None, ALU.subtract))
                        link(dve.tensor_tensor(best[:], best[:], keys2[:, :, 0], ALU.add))
                        link(dve.scalar_tensor_tensor(top2[:], best[:], SLOPE, best[:], ALU.mult, ALU.max))
                        link(dve.tensor_tensor(top2[:], top2[:], lone[:], ALU.add))
                        link(dve.tensor_tensor(alpha_col[:], keys2[:, :, 0], top2[:], ALU.subtract))
                        dve.scalar_tensor_tensor(beta_col[:], keys2[:, :, 0], SLOPE, top2[:], ALU.mult, ALU.subtract)\
                           .then_inc(cols_ready, 1)
                    elif kind == "top2":
                        if n == 0 and h == 0:
                            dve.wait_ge(rows_ready, T(4, 0))
                        dve.wait_ge(p2_slope, T(16, 8 * h + n + 1, -1))
                        link(dve.scalar_tensor_tensor(p_full[:, n % 3, :], alpha[:, nodes(h)], keys2[:, n, 1:2],
                                                      p_full[:, n % 3, :], ALU.add, ALU.max))
                        dve.scalar_tensor_tensor(p_full[:, n % 3, :], hidden[:, n, nodes(h)], NEG_INF,
                                                 p_full[:, n % 3, :], ALU.mult, ALU.add).then_inc(p2_masked, 1)
                    elif kind == "lo2":
                        dve.wait_ge(p2_hi, T(16, 8 * h + n + 1, -1))
                        dve.tensor_tensor(p_lo[:, slot(2, h, n), :], p_full[:, n % 3, :],
                                          p_hi[:, slot(2, h, n), :].bitcast(F32), ALU.subtract).then_inc(p2_ready, 1)
                    elif kind == "rsum2":
                        dve.wait_ge(p2_used, T(16, 8 * h + 8, -1))
                        if h == 1:
                            dve.wait_ge(att2_read, T(8, 4, -1))
                        dve.reciprocal(rsum2[:], ps[:, ATT2_BANKS[0]:ATT2_BANKS[0] + TH, O:O + 1]\
                                       .rearrange("p t c -> p (t c)")).then_inc(rsum2_ready, 1)
                    elif kind == "add2":
                        if h == 1 and n == 0:
                            dve.wait_ge(shift_ready, T(2, 1, -1))
                        dve.wait_ge(e2_done, T(8, 4 * h + n + 1, -1))
                        link(dve.scalar_tensor_tensor(u2(n), u2(n), 0.0, e2(n), ALU.max, ALU.add))
                        link(dve.tensor_tensor(u2(n), u2(n), act2[:, h * TH + n, :], ALU.add))
                        dve.wait_ge(y_loaded[h], T(16, 0))
                        link(dve.scalar_tensor_tensor(y[:, n, :], u2(n), 0.0, y[:, n, :], ALU.max, ALU.add))
                        link(dve.bn_stats(stats[:, n % 2, :], y[:, n, :]), alone=True)
                        dve.bn_aggr(moments[:, n, :], stats[:, n % 2, :]).then_inc(moments_ready, 1)
                    elif kind == "var2":
                        dve.wait_ge(moments_ready, T(8, 4 * h + 4, -1))
                        dve.tensor_scalar(var_eps[:], moments[:, :, 1], LN_EPS, None, ALU.add).then_inc(var_ready, 1)
                    elif kind == "shift2":
                        dve.wait_ge(rstd_ready, T(2, h + 1, -1))
                        dve.scalar_tensor_tensor(shift[:], moments[:, :, 0], -1.0, rstd[:], ALU.mult, ALU.mult)\
                           .then_inc(shift_ready, 1)
                assert links == links_of(steps), (links, links_of(steps))

            dve.wait_ge(w_ready, 5)
            run(FRONT, Turn(dve, -1), 0)
            base = links_of(FRONT)
            run(FIRST, Turn(dve, 0), base, first_turn=True)
            base += links_of(FIRST)
            with dve.Fori(1, NB - 1) as b:
                T = Turn(dve, b)
                run(STEADY, T, T(links_of(STEADY), base, -1))
            base += (NB - 2) * links_of(STEADY)
            run(FINISH, Turn(dve, NB - 1), base)
            run(LAST, Turn(dve, NB), base + links_of(FINISH))


NAMES = ["x", "adj", "L0_gnn_mlp1_w", "L0_gnn_mlp1_b", "L0_gnn_mlp2_w", "L0_gnn_mlp2_b", "L0_gnn_W_fc",
         "L0_gnn_a_fc", "L0_gnn_W_hand", "L0_gnn_a_hand"]


def kernel(**inputs):
    import numpy as np
    import concourse.bacc as bacc
    from concourse.bass_utils import run_bass_kernel_spmd

    nc = bacc.Bacc("TRN2", target_bir_lowering=False, num_devices=1)
    arrays, args = {}, []
    for name in NAMES:
        a = np.ascontiguousarray(inputs[name])
        arrays[name + "_dram"] = a
        args.append(nc.dram_tensor(name + "_dram", a.shape, mybir.dt.from_np(a.dtype), kind="ExternalInput").ap())
    out = nc.dram_tensor("out_dram", inputs["x"].shape, F32, kind="ExternalOutput").ap()
    build(nc, *args, out)
    result = run_bass_kernel_spmd(nc, [arrays], core_ids=[0])
    return result.results[0]["out_dram"]
```
